# Optimizing a Trainium2 kernel written in Bass

```python
import numpy as np
import jax
import jax.numpy as jnp

def _softmax(x, axis=-1):
    return jax.nn.softmax(x, axis=axis)

def _gelu(x):
    return jax.nn.gelu(x, approximate=True)

def _silu(x):
    return jax.nn.silu(x)

def _sigmoid(x):
    return jax.nn.sigmoid(x)

def _layernorm(x, axis=-1, eps=1e-05):
    m = jnp.mean(x, axis=axis, keepdims=True)
    v = jnp.var(x, axis=axis, keepdims=True)
    return (x - m) / jnp.sqrt(v + eps)

def _scatter_add(tgt, idx, src, axis=0):
    return tgt.at[idx].add(src)

def _segment_sum(src, seg, n):
    return jax.ops.segment_sum(src, seg, n)
kernel_name = 'mk_gnn_resnorm_d2_gnn_r16_554ca6'

def setup_inputs(seed: int=0):
    np.random.seed(seed)
    _w = jnp.asarray

    def _rec_inputs():
        import jax
        import jax.numpy as jnp
        _gk = jax.random.key(seed)
        x = -0.0003713 + 1 * jax.random.normal(jax.random.fold_in(_gk, 1), (6250, 256), jnp.float32)
        src = jax.random.randint(jax.random.fold_in(_gk, 2), (100000,), 0, 6250, jnp.int32)
        dst = jnp.minimum((6250 * jax.random.uniform(jax.random.fold_in(_gk, 3), (100000,)) ** 2.0).astype(jnp.int32), 99999)
        _o = jnp.argsort(dst, stable=True)
        src = src[_o]
        dst = dst[_o]
        edge_type_3 = jax.random.randint(jax.random.fold_in(_gk, 12), (100000,), 0, 3, jnp.int32)
        node_type_4 = jax.random.randint(jax.random.fold_in(_gk, 13), (6250,), 0, 4, jnp.int32)
        return (x, src, dst, edge_type_3, node_type_4)
    x, src, dst, edge_type_3, node_type_4 = _rec_inputs()

    def _L0_gnn_setup():
        import jax, jax.numpy as jnp
        import numpy as np
        N_NODES = 3125
        key = jax.random.key(seed)
        k1, k2, k3 = jax.random.split(key, 3)
        x = jax.random.normal(k1, (N_NODES, 256), dtype=jnp.float32)
        W = jax.random.normal(k2, (256, 256), dtype=jnp.float32) * (1.0 / np.sqrt(256))
        edge_index = jax.random.randint(k3, (2, 100000), 0, N_NODES, dtype=jnp.int64)
        return {'x': x, 'W': W, 'edge_index': edge_index}
    _L0_gnn_all = _L0_gnn_setup()
    _L0_gnn_in = {k: v for k, v in _L0_gnn_all.items() if k in ('W',)}
    del _L0_gnn_all

    def _L1_gnn_setup():
        import jax, jax.numpy as jnp
        import numpy as np
        import math
        L, H, HD, D = (3, 8, 32, 256)
        TN, TE = (4, 3)

        def _layer_norm(x, g, b, eps=1e-05):
            m = jnp.mean(x, axis=-1, keepdims=True)
            v = jnp.var(x, axis=-1, keepdims=True)
            return (x - m) / jnp.sqrt(v + eps) * g + b

        def _typed_transform(xh, W, types):
            out = jnp.zeros_like(xh)
            for t in range(W.shape[0]):
                y = jnp.einsum('mhd,hde->mhe', xh, W[t])
                out = jnp.where((types == t)[:, None, None], y, out)
            return out
        N, E = (1250, 20000)
        key = jax.random.key(seed)
        ks = jax.random.split(key, 16)
        inp = {}
        inp['x'] = jax.random.normal(ks[0], (N, D), dtype=jnp.float32)
        inp['edge_index'] = jax.random.randint(ks[1], (2, E), 0, N)
        inp['edge_type'] = jax.random.randint(ks[2], (E,), 0, TE)
        inp['node_type'] = jax.random.randint(ks[3], (N,), 0, TN)
        inp['W_Q'] = jax.random.normal(ks[4], (L, TN, H, HD, HD), dtype=jnp.float32) * 0.02
        inp['W_K'] = jax.random.normal(ks[5], (L, TN, H, HD, HD), dtype=jnp.float32) * 0.02
        inp['W_V'] = jax.random.normal(ks[6], (L, TN, H, HD, HD), dtype=jnp.float32) * 0.02
        inp['W_E'] = jax.random.normal(ks[7], (L, TE, H, HD, HD), dtype=jnp.float32) * 0.02
        inp['mu'] = jnp.ones((L, H, TE), dtype=jnp.float32)
        inp['Wo'] = jax.random.normal(ks[8], (L, D, D), dtype=jnp.float32) * 0.02
        inp['bo'] = jnp.zeros((L, D), dtype=jnp.float32)
        inp['ln1_g'] = jnp.ones((L, D), dtype=jnp.float32)
        inp['ln1_b'] = jnp.zeros((L, D), dtype=jnp.float32)
        inp['ln2_g'] = jnp.ones((L, D), dtype=jnp.float32)
        inp['ln2_b'] = jnp.zeros((L, D), dtype=jnp.float32)
        inp['w1'] = jax.random.normal(ks[9], (L, D, 4 * D), dtype=jnp.float32) * 0.02
        inp['b1'] = jnp.zeros((L, 4 * D), dtype=jnp.float32)
        inp['w2'] = jax.random.normal(ks[10], (L, 4 * D, D), dtype=jnp.float32) * 0.02
        inp['b2'] = jnp.zeros((L, D), dtype=jnp.float32)
        inp['out_g'] = jnp.ones((D,), dtype=jnp.float32)
        inp['out_b'] = jnp.zeros((D,), dtype=jnp.float32)
        return inp
    _L1_gnn_all = _L1_gnn_setup()
    _L1_gnn_in = {k: v for k, v in _L1_gnn_all.items() if k in ('W_Q', 'W_K', 'W_V', 'W_E', 'mu', 'Wo', 'bo', 'ln1_g', 'ln1_b', 'ln2_g', 'ln2_b', 'w1', 'b1', 'w2', 'b2', 'out_g', 'out_b')}
    del _L1_gnn_all
    return {'x': x, 'src': src, 'dst': dst, 'edge_type_3': edge_type_3, 'node_type_4': node_type_4, 'L0_gnn_W': _L0_gnn_in['W'], 'L1_gnn_W_Q': _L1_gnn_in['W_Q'], 'L1_gnn_W_K': _L1_gnn_in['W_K'], 'L1_gnn_W_V': _L1_gnn_in['W_V'], 'L1_gnn_W_E': _L1_gnn_in['W_E'], 'L1_gnn_mu': _L1_gnn_in['mu'], 'L1_gnn_Wo': _L1_gnn_in['Wo'], 'L1_gnn_bo': _L1_gnn_in['bo'], 'L1_gnn_ln1_g': _L1_gnn_in['ln1_g'], 'L1_gnn_ln1_b': _L1_gnn_in['ln1_b'], 'L1_gnn_ln2_g': _L1_gnn_in['ln2_g'], 'L1_gnn_ln2_b': _L1_gnn_in['ln2_b'], 'L1_gnn_w1': _L1_gnn_in['w1'], 'L1_gnn_b1': _L1_gnn_in['b1'], 'L1_gnn_w2': _L1_gnn_in['w2'], 'L1_gnn_b2': _L1_gnn_in['b2'], 'L1_gnn_out_g': _L1_gnn_in['out_g'], 'L1_gnn_out_b': _L1_gnn_in['out_b']}

def reference(x, src, dst, edge_type_3, node_type_4, L0_gnn_W, L1_gnn_W_Q, L1_gnn_W_K, L1_gnn_W_V, L1_gnn_W_E, L1_gnn_mu, L1_gnn_Wo, L1_gnn_bo, L1_gnn_ln1_g, L1_gnn_ln1_b, L1_gnn_ln2_g, L1_gnn_ln2_b, L1_gnn_w1, L1_gnn_b1, L1_gnn_w2, L1_gnn_b2, L1_gnn_out_g, L1_gnn_out_b):
    import jax
    import jax.numpy as jnp

    def _L0_gnn_ref(x, W, edge_index):
        import jax, jax.numpy as jnp
        import numpy as np
        N_NODES = 3125
        N = x.shape[0]
        src, dst = (edge_index[0], edge_index[1])
        h = x @ W
        deg = jax.ops.segment_sum(jnp.ones_like(dst, dtype=h.dtype), dst, num_segments=N)
        deg_inv_sqrt = jnp.where(deg > 0, jax.lax.rsqrt(jnp.maximum(deg, 1)), 0.0)
        norm = deg_inv_sqrt[src] * deg_inv_sqrt[dst]
        msgs = h[src] * norm[:, None]
        out = jax.ops.segment_sum(msgs, dst, num_segments=N)
        return out

    def _L1_gnn_ref(x, edge_index, edge_type, node_type, W_Q, W_K, W_V, W_E, mu, Wo, bo, ln1_g, ln1_b, ln2_g, ln2_b, w1, b1, w2, b2, out_g, out_b):
        import jax, jax.numpy as jnp
        import numpy as np
        import math
        L, H, HD, D = (3, 8, 32, 256)
        TN, TE = (4, 3)

        def _layer_norm(x, g, b, eps=1e-05):
            m = jnp.mean(x, axis=-1, keepdims=True)
            v = jnp.var(x, axis=-1, keepdims=True)
            return (x - m) / jnp.sqrt(v + eps) * g + b

        def _typed_transform(xh, W, types):
            out = jnp.zeros_like(xh)
            for t in range(W.shape[0]):
                y = jnp.einsum('mhd,hde->mhe', xh, W[t])
                out = jnp.where((types == t)[:, None, None], y, out)
            return out
        N = x.shape[0]
        src, dst = (edge_index[0], edge_index[1])
        scale = math.sqrt(HD)
        for l in range(L):
            xh = x.reshape(N, H, HD)
            Q = _typed_transform(xh, W_Q[l], node_type)
            K = _typed_transform(xh, W_K[l], node_type)
            V = _typed_transform(xh, W_V[l], node_type)
            q_dst = Q[dst]
            kt = _typed_transform(K[src], W_E[l], edge_type)
            scores = jnp.sum(q_dst * kt, axis=-1) / scale
            scores = scores * mu[l].T[edge_type]
            m = jax.ops.segment_max(scores, dst, num_segments=N)
            m = jnp.maximum(m, -1000000000.0)
            e = jnp.exp(scores - m[dst])
            s = jax.ops.segment_sum(e, dst, num_segments=N)
            w = e / (s[dst] + 1e-10)
            agg = jax.ops.segment_sum(V[src] * w[..., None], dst, num_segments=N)
            attn = agg.reshape(N, D) @ Wo[l] + bo[l]
            x = _layer_norm(x + attn, ln1_g[l], ln1_b[l])
            h = jax.nn.gelu(x @ w1[l] + b1[l], approximate=False) @ w2[l] + b2[l]
            x = _layer_norm(x + h, ln2_g[l], ln2_b[l])
        return _layer_norm(x, out_g, out_b)
    edge_index = jnp.stack([src, dst])
    x = _layernorm(x + _L0_gnn_ref(x, L0_gnn_W, edge_index), axis=-1)
    x = _layernorm(x + _L1_gnn_ref(x, edge_index, edge_type_3, node_type_4, L1_gnn_W_Q, L1_gnn_W_K, L1_gnn_W_V, L1_gnn_W_E, L1_gnn_mu, L1_gnn_Wo, L1_gnn_bo, L1_gnn_ln1_g, L1_gnn_ln1_b, L1_gnn_ln2_g, L1_gnn_ln2_b, L1_gnn_w1, L1_gnn_b1, L1_gnn_w2, L1_gnn_b2, L1_gnn_out_g, L1_gnn_out_b), axis=-1)
    return x

_drawn_inputs = setup_inputs


def setup_inputs(seed=0):
    import zlib

    import numpy as np

    out = dict(_drawn_inputs(seed))
    spreads = {'L1_gnn_mu': (1.0, 0.6),
     'L1_gnn_bo': (0.0, 0.1),
     'L1_gnn_ln1_g': (1.0, 0.2),
     'L1_gnn_ln1_b': (0.0, 0.1),
     'L1_gnn_ln2_g': (1.0, 0.2),
     'L1_gnn_ln2_b': (0.0, 0.1),
     'L1_gnn_b1': (0.0, 0.1),
     'L1_gnn_b2': (0.0, 0.1),
     'L1_gnn_out_g': (1.0, 0.2),
     'L1_gnn_out_b': (0.0, 0.1)}
    factors = {'L1_gnn_W_Q': 8.0,
     'L1_gnn_W_K': 8.0,
     'L1_gnn_W_V': 5.497,
     'L1_gnn_W_E': 8.0,
     'L1_gnn_Wo': 5.616}
    for name, (base, spread) in spreads.items():
        noise = np.random.default_rng([zlib.crc32(name.encode()), seed]).standard_normal(out[name].shape)
        drawn = base * np.exp(spread * noise) if base else spread * noise
        out[name] = jnp.asarray(drawn.astype(out[name].dtype))
    for name, factor in factors.items():
        out[name] = (out[name] * factor).astype(out[name].dtype)
    return out
```

```python
import concourse.bass as bass
from concourse import mybir
from contextlib import ExitStack

F32 = mybir.dt.float32
I32 = mybir.dt.int32
BF16 = mybir.dt.bfloat16
ALU = mybir.AluOpType
ACT = mybir.ActivationFunctionType
AX = mybir.AxisListType
PE_ENGINE = mybir.EngineType.PE
DVE_ENGINE = mybir.EngineType.DVE

P = 128
N, E, D = 6250, 100000, 256
LAYERS, HEADS, HD = 3, 8, 32
NODE_TYPES, EDGE_TYPES = 4, 3
HIDDEN = 4 * D
WINDOWS = 50
NPAD = WINDOWS * P
GROUP = 2 * P
GROUPS = -(-E // GROUP)
CHUNKS = -(-(GROUPS + 1) // P)
NO_GROUP = 440
BLOCK = 8
TILES = 2 * BLOCK
PAIRS = 448
BLOCKS = PAIRS // BLOCK
ROUNDS = BLOCKS // 2
RING = 16
PASS_LANDED = 32 * ROUNDS
assert GROUPS + WINDOWS - 1 <= PAIRS and GROUPS <= NO_GROUP < CHUNKS * P
NOWHERE = 8191
BIG = 3.0e38
FLOOR = -1.0e9
EPS = 1e-5
SOFT_EPS = 1e-10

ROW = 2 * D
SLOT = ROW + HEADS
UROW = D + HEADS
PROJ = 2 + EDGE_TYPES

REC_PEN, REC_FIRST, REC_LAST, REC_CROSS = 0, 129, 257, 385
CROSS = 2 * TILES + 1
REC_CARRY = REC_CROSS + 2 * CROSS
REC_PLACE = REC_CARRY + 1
REC = REC_PLACE + TILES


def need(eng, sem, value):
    if isinstance(value, int) and value <= 0:
        return
    eng.wait_ge(sem, value)


def need_apart(eng, sem, value):
    if isinstance(value, int) and value <= 0:
        return
    eng.wait_ge(sem, value)
    eng.nop(nofuse=True)


def end_phase(nc, sems):
    for s in sems:
        nc.sync.sem_clear(s)
    nc.all_engine_barrier()


def load_words(nc, row, engine, start, count):
    _, words = nc.values_load_multi_w_load_instructions(
        row[0:1, bass.ds(start, count)], [engine],
        skip_runtime_bounds_check_because="windows are clamped to 0..WINDOWS-1 where they are computed")
    return words


RSQRT_SIGNALS = 11
SEED = 0x5F3759DF


def reciprocal_sqrt(v, value, root, bits, half, done, count):
    at = [count]

    def then(inst):
        at[0] += 1
        inst.then_inc(done, 1)
        v.wait_ge(done, at[0])

    then(v.tensor_single_scalar(bits, value.bitcast(I32), 1, ALU.arith_shift_right))
    then(v.tensor_scalar(root.bitcast(I32), bits, -1.0, float(SEED), ALU.mult, ALU.add))
    for _ in range(3):
        then(v.tensor_tensor(half, value, root, ALU.mult))
        then(v.scalar_tensor_tensor(out=half, in0=half, scalar=-0.5, in1=root, op0=ALU.mult, op1=ALU.mult))
        then(v.scalar_tensor_tensor(out=root, in0=half, scalar=1.5, in1=root, op0=ALU.add, op1=ALU.mult))


class Shared:
    pass


def constants(nc, g):
    with ExitStack() as ctx:
        diff = ctx.enter_context(nc.sbuf_tensor("diff", [P, P], I32))
        type_rows = ctx.enter_context(nc.sbuf_tensor("type_rows", [WINDOWS, P], I32))
        type_rows_f = ctx.enter_context(nc.sbuf_tensor("type_rows_f", [WINDOWS, P], F32))
        type_col = ctx.enter_context(nc.sbuf_tensor("type_col", [P, WINDOWS], F32))
        made = ctx.enter_context(nc.semaphore("const_made"))
        masks = ctx.enter_context(nc.semaphore("const_masks"))
        cleared = ctx.enter_context(nc.semaphore("const_cleared"))
        loaded = ctx.enter_context(nc.semaphore("const_loaded"))
        turned = ctx.enter_context(nc.semaphore("const_turned"))
        whole = N // P
        with nc.Block() as block:

            @block.sync
            def _(sp):
                sp.wait_ge(cleared, 1)
                sp.dma_start(type_rows[0:whole, :],
                             g.node_type[0:whole * P].rearrange("(w p) -> w p", p=P)).then_inc(loaded, 16)
                sp.dma_start(type_rows[whole:whole + 1, 0:N - whole * P],
                             g.node_type[whole * P:N].rearrange("(w p) -> w p", w=1)).then_inc(loaded, 16)

            @block.tensor
            def _(t):
                t.wait_ge(made, 6)
                t.wait_ge(masks, 3)
                t.transpose(g.ps[:, 0, 0:WINDOWS], type_rows_f[:], g.ident[0:WINDOWS, 0:WINDOWS]).then_inc(turned, 1)

            @block.gpsimd
            def _(pool):
                nc.gpsimd.memset(g.ident[:], 0.0).then_inc(made, 1)
                nc.gpsimd.memset(g.tile_hot[:], 1.0).then_inc(made, 1)
                pool.wait_ge(made, 2)
                nc.gpsimd.affine_select(out=g.ident[:], in_=g.ident[:], compare_op=ALU.not_equal, fill=1.0,
                                        base=0, pattern=[[-1, P]], channel_multiplier=1).then_inc(made, 1)
                nc.gpsimd.affine_select(out=g.tile_hot[:], in_=g.tile_hot[:], compare_op=ALU.is_ge, fill=0.0,
                                        base=0, pattern=[[-HEADS, TILES]], channel_multiplier=1).then_inc(made, 1)
                pool.wait_ge(made, 4)
                nc.gpsimd.affine_select(out=g.tile_hot[:], in_=g.tile_hot[:], compare_op=ALU.is_ge, fill=0.0,
                                        base=HEADS - 1, pattern=[[HEADS, TILES]],
                                        channel_multiplier=-1).then_inc(made, 1)
                nc.gpsimd.iota(g.iota[:], [[1, P]], 0, 0, allow_small_or_imprecise_dtypes=True)
                nc.gpsimd.iota(g.pair_iota[:], [[P, 4]], 0, 1, allow_small_or_imprecise_dtypes=True)
                nc.gpsimd.iota(diff[:], [[-1, P]], P, 1).then_inc(made, 1)

            @block.vector
            def _(v):
                v.memset(type_rows[:], 0).then_inc(cleared, 1)
                v.memset(g.ones[:], 1.0)
                v.memset(g.zeros[:], 0.0)
                v.memset(g.sums[:], 0.0)
                v.wait_ge(made, 6)
                v.tensor_single_scalar(diff[:], diff[:], HEADS - 1, ALU.bitwise_and).then_inc(masks, 1)
                v.wait_ge(masks, 1)
                v.tensor_single_scalar(g.same_head[:], diff[:], 0, ALU.is_equal).then_inc(masks, 1)
                v.wait_ge(loaded, 32)
                v.tensor_copy(type_rows_f[:], type_rows[:]).then_inc(masks, 1)
                v.wait_ge(turned, 1)
                v.tensor_copy(type_col[:], g.ps[:, 0, 0:WINDOWS]).then_inc(masks, 1)
                v.wait_ge(masks, 4)
                for k in range(NODE_TYPES):
                    v.tensor_scalar(g.type_hot[:, :, k], type_col[:], float(k), None, ALU.is_equal)

        end_phase(nc, [made, masks, cleared, loaded, turned])


def index_pairs(nc, g):
    with ExitStack() as ctx:
        def sb(name, shape, dt=F32):
            return ctx.enter_context(nc.sbuf_tensor(name, shape, dt))

        def sem(name):
            s = ctx.enter_context(nc.semaphore(name))
            sems.append(s)
            return s

        sems = []
        raw = sb("raw", [P, 3, CHUNKS, GROUP], I32)
        part = sb("part", [P, 2, CHUNKS, GROUP], I32)
        val = sb("val", [P, 3, CHUNKS, GROUP])
        typ = sb("typ", [P, CHUNKS, GROUP])
        partf = sb("partf", [P, 2, CHUNKS, GROUP])
        cols = sb("cols", [P, 2, 2 * CHUNKS, P])
        place_hot = sb("place_hot", [P, 2, 16, P], BF16)
        window_hot = sb("window_hot", [P, 2, 16, WINDOWS], BF16)
        deg = sb("deg", [P, WINDOWS])
        cnt = sb("cnt", [P, WINDOWS])
        work = sb("work", [P, 12, WINDOWS])
        ints = sb("ints", [P, 2, WINDOWS], I32)
        mask = sb("mask", [P, 4, 4, WINDOWS])
        pv = sb("pv", [P, 12, 4])
        diag = sb("diag", [P, 12, P])
        prow = sb("prow", [P, 3, 512])
        pick = sb("pick", [P, CHUNKS, 512])
        got = sb("got", [P, 3, 512, 2])
        place = sb("place", [P, 512, 2])
        flag = sb("flag", [P, 3, 512, 2])
        loaded, pad_set, vec, turned, columned, hot_ready, hot_used = (
            sem("ix_loaded"), sem("ix_pad"), sem("ix_vec"), sem("ix_turned"), sem("ix_columned"),
            sem("ix_hot"), sem("ix_hot_used"))
        parted, counted, deg_ready, diag_ready, spread, pick_ready, picked, evac, stored, idx_ready = (
            sem("ix_parted"), sem("ix_counted"), sem("ix_deg"), sem("ix_diag"), sem("ix_spread"),
            sem("ix_pick"), sem("ix_picked"), sem("ix_evac"), sem("ix_stored"), sem("ix_idx"))
        ps = g.ps
        full = (E // GROUP) // P
        tail = E // GROUP - full * P
        rest = E - (E // GROUP) * GROUP
        HIST = full * 2 * P // 16
        with nc.Block() as block:

            @block.sync
            def _(sp):
                for a, src in enumerate((g.dst, g.src, g.edge_type)):
                    sp.dma_start(raw[:, a, 0:full, :],
                                 src[0:full * P * GROUP].rearrange("(c s e) -> s c e", c=full, s=P)).then_inc(loaded, 16)
                sp.wait_ge(pad_set, 2)
                for a, src in enumerate((g.dst, g.src, g.edge_type)):
                    sp.dma_start(raw[0:tail, a, full, :],
                                 src[full * P * GROUP:E - rest].rearrange("(s e) -> s e", e=GROUP)).then_inc(loaded, 16)
                    sp.dma_start(raw[tail:tail + 1, a, full, 0:rest],
                                 src[E - rest:E].rearrange("(s e) -> s e", s=1)).then_inc(loaded, 16)
                sp.dma_start(g.x_d[0:N, :], g.x).then_inc(stored, 16)
                sp.dma_start(g.x_d[N:N + P, :], g.zeros[:, 0:D]).then_inc(stored, 16)
                sp.dma_start(g.x_d[N + P:NPAD, :], g.zeros[0:NPAD - N - P, 0:D]).then_inc(stored, 16)
                sp.wait_ge(idx_ready, 1)
                for kind in range(2):
                    for half in range(2):
                        b0, b1 = half * BLOCKS // 2, (half + 1) * BLOCKS // 2
                        sp.dma_start(g.idx_d[kind, b0:b1].rearrange("b p t -> p b t"),
                                     g.idx[:, kind, b0:b1, :]).then_inc(stored, 16)
                sp.wait_ge(stored, 16 * 7)

            @block.tensor
            def _(t):
                t.wait_ge(parted, 1)
                for a in range(2):
                    for half in range(2):
                        k = 2 * a + half
                        for q in range(4):
                            c, j = divmod(4 * half + q, 2)
                            tr = t.transpose(ps[:, k, q * P:(q + 1) * P], partf[:, a, c, j * P:(j + 1) * P], g.ident[:])
                        tr.then_inc(turned, 1)
                def histogram(turn, buf, first, last):
                    need(t, hot_ready, turn + 1)
                    for u in range(16):
                        mm = t.matmul(ps[:, 4, 0:WINDOWS], place_hot[:, buf, u, :], window_hot[:, buf, u, :],
                                      start=first and u == 0, stop=last and u == 15, skip_group_check=True)
                    mm.then_inc(hot_used, 1)

                histogram(0, 0, True, False)
                histogram(1, 1, False, False)
                with t.Fori(1, HIST // 2) as i:
                    histogram(2 * i, 0, False, False)
                    histogram(2 * i + 1, 1, False, False)
                histogram(HIST, 0, False, False)
                histogram(HIST + 1, 1, False, True)
                t.wait_ge(deg_ready, 1)
                t.matmul(ps[:, 5, 0:WINDOWS], g.ones[:, 0:P], cnt[:], start=True, stop=True).then_inc(counted, 1)
                t.wait_ge(diag_ready, 1)
                for a in range(3):
                    for q in range(4):
                        mm = t.matmul(ps[:, a, q * P:(q + 1) * P], g.ones[:, 0:P], diag[:, 4 * a + q, :],
                                      start=True, stop=True)
                    mm.then_inc(spread, 1)
                t.wait_ge(pick_ready, 1)
                for a in range(3):
                    for j in range(2):
                        k = 2 * a + j
                        for c in range(CHUNKS):
                            mm = t.matmul(ps[:, 2 + k, :], val[:, a, c, j * P:(j + 1) * P], pick[:, c, :],
                                          start=c == 0, stop=c == CHUNKS - 1)
                        mm.then_inc(picked, 1)

            @block.scalar
            def _(act):
                for k in range(4):
                    a, half = divmod(k, 2)
                    act.wait_ge(turned, k + 1)
                    act.copy(cols[:, a, 4 * half:4 * half + 4, :],
                             ps[:, k, :].rearrange("p (q s) -> p q s", q=4)).then_inc(columned, 1)
                for k in range(6):
                    a, j = divmod(k, 2)
                    act.wait_ge(picked, k + 1)
                    act.copy(got[:, a, :, j], ps[:, 2 + k, :]).then_inc(evac, 1)

            @block.vector
            def _(v):
                steps = [0]

                def then(inst):
                    steps[0] += 1
                    inst.then_inc(vec, 1)
                    v.wait_ge(vec, steps[0])

                v.memset(raw[:, 0, full, :], NOWHERE).then_inc(pad_set, 1)
                v.memset(raw[:, 1:3, full, :], 0).then_inc(pad_set, 1)
                v.wait_ge(loaded, 16 * 9)
                v.tensor_single_scalar(part[:, 0], raw[:, 0], 7, ALU.arith_shift_right)
                then(v.tensor_single_scalar(part[:, 1], raw[:, 0], P - 1, ALU.bitwise_and))
                v.tensor_copy(partf[:], part[:]).then_inc(parted, 1)
                v.tensor_copy(val[:, 0:2], raw[:, 0:2])
                then(v.tensor_copy(typ[:], raw[:, 2]))
                v.scalar_tensor_tensor(out=val[:, 2], in0=typ[:], scalar=float(NPAD), in1=val[:, 1],
                                       op0=ALU.mult, op1=ALU.add)
                v.wait_ge(columned, 4)

                def hots(turn, buf, c0, s0):
                    need(v, hot_used, turn - 1)
                    v.tensor_tensor(place_hot[:, buf], cols[:, 1, c0, s0][:, :, None].to_broadcast([P, 16, P]),
                                    g.iota[:, None, :].to_broadcast([P, 16, P]), ALU.is_equal)
                    v.tensor_tensor(window_hot[:, buf], cols[:, 0, c0, s0][:, :, None].to_broadcast([P, 16, WINDOWS]),
                                    g.iota[:, None, 0:WINDOWS].to_broadcast([P, 16, WINDOWS]),
                                    ALU.is_equal).then_inc(hot_ready, 1)

                hots(0, 0, 0, slice(0, 16))
                hots(1, 1, 0, slice(16, 32))
                flat = [cols[:, a].rearrange("p c s -> p (c s)") for a in range(2)]
                with v.Fori(1, HIST // 2) as i:
                    for b in range(2):
                        v.wait_ge(hot_used, 2 * i + b - 1)
                        v.tensor_tensor(place_hot[:, b],
                                        flat[1][:, bass.ds(32 * i + 16 * b, 16)][:, :, None].to_broadcast([P, 16, P]),
                                        g.iota[:, None, :].to_broadcast([P, 16, P]), ALU.is_equal)
                        v.tensor_tensor(window_hot[:, b],
                                        flat[0][:, bass.ds(32 * i + 16 * b, 16)][:, :, None].to_broadcast([P, 16, WINDOWS]),
                                        g.iota[:, None, 0:WINDOWS].to_broadcast([P, 16, WINDOWS]),
                                        ALU.is_equal).then_inc(hot_ready, 1)
                hots(HIST, 0, 2 * full, slice(0, 16))
                hots(HIST + 1, 1, 2 * full + 1, slice(0, 16))
                v.wait_ge(hot_used, HIST + 2)
                then(v.tensor_copy(deg[:], ps[:, 4, 0:WINDOWS]))
                then(v.tensor_scalar(work[:, 0], deg[:], 1.0, None, ALU.max))
                v.tensor_copy(cnt[:], deg[:]).then_inc(deg_ready, 1)
                reciprocal_sqrt(v, work[:, 0], work[:, 1], ints[:, 0], work[:, 11], vec, steps[0])
                steps[0] += RSQRT_SIGNALS
                v.scalar_tensor_tensor(out=g.dis[:], in0=deg[:], scalar=0.0, in1=work[:, 1],
                                       op0=ALU.is_gt, op1=ALU.mult)
                v.wait_ge(counted, 1)
                COUNT, END, START, G0, G1, NP, PEND, PST, OFF = 2, 3, 4, 5, 6, 7, 8, 9, 10
                then(v.tensor_copy(work[:, COUNT], ps[:, 5, 0:WINDOWS]))
                then(v.tensor_tensor_scan(work[:, END], work[:, COUNT], g.zeros[:, 0:WINDOWS], 0.0, ALU.add, ALU.add))
                then(v.tensor_tensor(work[:, START], work[:, END], work[:, COUNT], ALU.subtract))
                v.tensor_copy(ints[:, 0], work[:, START])
                then(v.tensor_scalar(ints[:, 1], work[:, END], -1.0, None, ALU.add))
                v_ints = ints[:].rearrange("p a w -> p (a w)")
                then(v.tensor_single_scalar(v_ints, v_ints, 8, ALU.arith_shift_right))
                then(v.tensor_copy(work[:, G0:G1 + 1], ints[:]))
                then(v.tensor_tensor(work[:, NP], work[:, G1], work[:, G0], ALU.subtract))
                then(v.scalar_tensor_tensor(out=work[:, NP], in0=work[:, COUNT], scalar=0.0, in1=work[:, NP],
                                            op0=ALU.is_gt, op1=ALU.mult))
                then(v.tensor_scalar(work[:, NP], work[:, NP], 1.0, None, ALU.add))
                then(v.tensor_tensor_scan(work[:, PEND], work[:, NP], g.zeros[:, 0:WINDOWS], 0.0, ALU.add, ALU.add))
                then(v.tensor_tensor(work[:, PST], work[:, PEND], work[:, NP], ALU.subtract))
                then(v.tensor_scalar(work[:, G0], work[:, G0], float(GROUPS - 1), None, ALU.min))
                then(v.tensor_tensor(work[:, OFF], work[:, G0], work[:, PST], ALU.subtract))
                shape = [P, 4, WINDOWS]

                def windows_row(k):
                    return work[:, k, None, :].to_broadcast(shape)

                pairs_col = g.pair_iota[:, :, None].to_broadcast(shape)
                then(v.tensor_tensor(mask[:, 0], windows_row(PEND), pairs_col, ALU.is_le))
                then(v.tensor_reduce(pv[:, 0], mask[:, 0], AX.X, ALU.add))
                then(v.tensor_tensor(mask[:, 1], g.iota[:, None, 0:WINDOWS].to_broadcast(shape),
                                     pv[:, 0, :, None].to_broadcast(shape), ALU.is_equal))
                v.tensor_tensor(mask[:, 2], mask[:, 1], windows_row(OFF), ALU.mult)
                then(v.tensor_tensor(mask[:, 3], mask[:, 1], windows_row(PST), ALU.mult))
                v.tensor_reduce(pv[:, 1], mask[:, 2], AX.X, ALU.add)
                then(v.tensor_reduce(pv[:, 2], mask[:, 3], AX.X, ALU.add))
                GRP, WIN, KEEP = 8, 9, 10
                then(v.tensor_tensor(pv[:, 3], pv[:, 1], g.pair_iota[:], ALU.add))
                then(v.tensor_scalar(pv[:, 4], pv[:, 0], float(WINDOWS), None, ALU.is_lt))
                then(v.tensor_scalar(pv[:, 3], pv[:, 3], -float(NO_GROUP), None, ALU.add))
                then(v.tensor_tensor(pv[:, 3], pv[:, 3], pv[:, 4], ALU.mult))
                v.tensor_scalar(pv[:, GRP], pv[:, 3], float(NO_GROUP), None, ALU.add)
                v.tensor_scalar(pv[:, WIN], pv[:, 0], float(WINDOWS - 1), None, ALU.min)
                then(v.tensor_tensor(pv[:, KEEP], pv[:, 2], g.pair_iota[:], ALU.not_equal))
                for k in range(12):
                    a, q = divmod(k, 4)
                    d = v.tensor_scalar(diag[:, k], g.ident[:], pv[:, GRP + a, q:q + 1], None, ALU.mult)
                d.then_inc(diag_ready, 1)
                v.wait_ge(spread, 3)
                then(v.tensor_copy(prow[:], ps[:, 0:3, :]))
                for c in range(CHUNKS):
                    d = v.tensor_scalar(pick[:, c], prow[:, 0], g.pair_iota[:, c:c + 1], None, ALU.is_equal)
                d.then_inc(pick_ready, 1)
                v.tensor_copy(g.keep[:], prow[:, 2, 0:PAIRS])
                v.memset(g.window_rows[:], 0).then_inc(pad_set, 1)
                v.wait_ge(pad_set, 3)
                for k, shift in enumerate(g.shifts):
                    v.tensor_copy(g.window_rows[0:1, k, shift:shift + PAIRS], prow[0:1, 1, 0:PAIRS])
                v.memset(g.before[:, 0:1], 1.0)
                v.tensor_scalar(g.before[:, 1:BLOCKS], prow[:, 1, BLOCK - 1:PAIRS - 1:BLOCK], -float(P), 1.0,
                                ALU.mult, ALU.add)
                v.wait_ge(evac, 6)
                then(v.scalar_tensor_tensor(out=place[:], in0=prow[:, 1, :, None].to_broadcast([P, 512, 2]),
                                            scalar=-float(P), in1=got[:, 0], op0=ALU.mult, op1=ALU.add))
                in_block = g.idx[:].rearrange("p k b t -> p k (b t)")
                v.tensor_copy(in_block[:, 0], got[:, 1].rearrange("p q j -> p (q j)")[:, 0:2 * PAIRS])
                v.tensor_copy(in_block[:, 1], got[:, 2].rearrange("p q j -> p (q j)")[:, 0:2 * PAIRS]).then_inc(idx_ready, 1)
                pl = place[:].rearrange("p q j -> p (q j)")[:, 0:2 * PAIRS]
                v.tensor_scalar(g.minus_place[:], pl, -1.0, None, ALU.mult)
                fl = [flag[:, k].rearrange("p q j -> p (q j)")[:, 0:2 * PAIRS] for k in range(3)]
                then(v.tensor_scalar(fl[0], pl, 0.0, None, ALU.is_ge))
                then(v.scalar_tensor_tensor(out=fl[1], in0=pl, scalar=float(P), in1=fl[0], op0=ALU.is_lt, op1=ALU.mult))
                then(v.scalar_tensor_tensor(out=fl[2], in0=got[:, 0].rearrange("p q j -> p (q j)")[:, 0:2 * PAIRS],
                                            scalar=1.0, in1=fl[1], op0=ALU.add, op1=ALU.mult))
                then(v.tensor_scalar(g.key[:], fl[2], -1.0, None, ALU.add))

        end_phase(nc, sems)


def block_records(nc, g):
    QUAD = 4
    TURNS = BLOCKS // QUAD
    with ExitStack() as ctx:
        def sb(name, shape, dt=F32):
            return ctx.enter_context(nc.sbuf_tensor(name, shape, dt))

        def sem(name):
            s = ctx.enter_context(nc.semaphore(name))
            sems.append(s)
            return s

        sems = []
        by_head = sb("by_head", [P, QUAD * TILES, HEADS])
        kt = sb("kt", [P, QUAD, P])
        ends = sb("ends", [P, QUAD, CROSS])
        last_key = sb("last_key", [P, 1])
        carry = sb("carry", [P, 2, QUAD])
        rec = sb("rec", [P, QUAD, REC])
        keyed, turned, copied, ends_ready, crossed, vec, rec_ready, stored, rec_free = (
            sem("br_keyed"), sem("br_turned"), sem("br_copied"), sem("br_ends"), sem("br_crossed"),
            sem("br_vec"), sem("br_rec"), sem("br_stored"), sem("br_free"))
        with nc.Block() as block:

            @block.sync
            def _(sp):
                sp.sem_inc(rec_free, 1)
                with sp.Fori(0, TURNS) as i:
                    sp.wait_ge(rec_ready, i + 1)
                    sp.dma_start(g.rec_d[bass.ds(QUAD * i, QUAD)].rearrange("b p r -> p b r"), rec[:]).then_inc(stored, 16)
                    sp.wait_ge(stored, 16 * i + 16)
                    sp.sem_inc(rec_free, 1)

            @block.tensor
            def _(t):
                with t.Fori(0, TURNS) as i:
                    t.wait_ge(keyed, i + 1)
                    for q in range(QUAD):
                        tr = t.transpose(g.ps[:, 0, q * P:(q + 1) * P],
                                         by_head[:, q * TILES:(q + 1) * TILES, :].rearrange("p t h -> p (t h)"), g.ident[:])
                    tr.then_inc(turned, 1)
                    t.wait_ge(ends_ready, i + 1)
                    t.matmul(g.ps[:, 1, 0:QUAD * CROSS], g.same_head[:], ends[:].rearrange("p q c -> p (q c)"),
                             start=True, stop=True).then_inc(crossed, 1)

            @block.scalar
            def _(act):
                with act.Fori(0, TURNS) as i:
                    act.wait_ge(turned, i + 1)
                    act.copy(kt[:], g.ps[:, 0, :].rearrange("p (q e) -> p q e", q=QUAD)).then_inc(copied, 1)

            @block.vector
            def _(v):
                v.memset(last_key[:], -2.0)
                v.memset(rec[:], -BIG).then_inc(vec, 1)
                v.wait_ge(vec, 1)
                STEPS = 5
                with v.Fori(0, TURNS) as i:
                    steps = [1]

                    def then(inst):
                        steps[0] += 1
                        inst.then_inc(vec, 1)
                        v.wait_ge(vec, STEPS * i + steps[0])

                    tiles = g.key[:, bass.ds(QUAD * TILES * i, QUAD * TILES)]
                    v.tensor_copy(by_head[:], tiles[:, :, None].to_broadcast([P, QUAD * TILES, HEADS])).then_inc(keyed, 1)
                    v.wait_ge(copied, i + 1)
                    hot = g.tile_hot[:, None, :].to_broadcast([P, QUAD, TILES])
                    v.tensor_tensor(ends[:, :, 0:TILES], hot, kt[:, :, 0:1].to_broadcast([P, QUAD, TILES]), ALU.mult)
                    v.tensor_tensor(ends[:, :, TILES:2 * TILES], hot, kt[:, :, P - 1:P].to_broadcast([P, QUAD, TILES]),
                                    ALU.mult)
                    v.tensor_tensor(ends[:, 0, CROSS - 1:CROSS], g.tile_hot[:, TILES - 1:TILES], last_key[:], ALU.mult)
                    then(v.tensor_tensor(ends[:, 1:QUAD, CROSS - 1:CROSS],
                                         g.tile_hot[:, None, TILES - 1:TILES].to_broadcast([P, QUAD - 1, 1]),
                                         kt[:, 0:QUAD - 1, P - 1:P], ALU.mult))
                    v.tensor_copy(last_key[:], kt[:, QUAD - 1, P - 1:P]).then_inc(ends_ready, 1)
                    v.wait_ge(rec_free, i + 1)
                    v.tensor_tensor(rec[:, :, REC_PEN + 1:REC_PEN + P], kt[:, :, 1:P], kt[:, :, 0:P - 1], ALU.not_equal)
                    v.tensor_tensor(rec[:, :, REC_FIRST:REC_FIRST + P], kt[:], kt[:, :, 0:1].to_broadcast([P, QUAD, P]),
                                    ALU.not_equal)
                    v.tensor_tensor(rec[:, :, REC_LAST:REC_LAST + P], kt[:], kt[:, :, P - 1:P].to_broadcast([P, QUAD, P]),
                                    ALU.not_equal)
                    v.wait_ge(crossed, i + 1)
                    cross = g.ps[:, 1, 0:QUAD * CROSS].rearrange("p (q c) -> p q c", q=QUAD)
                    v.tensor_tensor(rec[:, :, REC_CROSS:REC_CROSS + CROSS], cross,
                                    kt[:, :, 0:1].to_broadcast([P, QUAD, CROSS]), ALU.not_equal)
                    v.tensor_tensor(rec[:, :, REC_CROSS + CROSS:REC_CARRY], cross,
                                    kt[:, :, P - 1:P].to_broadcast([P, QUAD, CROSS]), ALU.not_equal)
                    then(v.tensor_tensor(carry[:, 0], cross[:, :, CROSS - 1], g.before[:, bass.ds(QUAD * i, QUAD)],
                                         ALU.add))
                    then(v.tensor_tensor(carry[:, 1], cross[:, :, CROSS - 1], kt[:, :, 0], ALU.is_equal))
                    then(v.tensor_tensor(carry[:, 0], carry[:, 0], carry[:, 1], ALU.mult))
                    v.tensor_scalar(rec[:, :, REC_CARRY], carry[:, 0], -1.0, None, ALU.add)
                    places = g.minus_place[:, bass.ds(QUAD * TILES * i, QUAD * TILES)]
                    v.tensor_copy(rec[:, :, REC_PLACE:REC], places.rearrange("p (q t) -> p q t", q=QUAD))
                    then(v.tensor_scalar(rec[:, :, REC_PEN + 1:REC_PEN + P], rec[:, :, REC_PEN + 1:REC_PEN + P], -BIG,
                                         None, ALU.mult))
                    v.tensor_scalar(rec[:, :, REC_FIRST:REC_CARRY], rec[:, :, REC_FIRST:REC_CARRY], -BIG, None,
                                    ALU.mult).then_inc(rec_ready, 1)
                    assert steps[0] == 1 + STEPS

        end_phase(nc, sems)


def gcn_edges(nc, g):
    with ExitStack() as ctx:
        def sb(name, shape, dt=F32):
            return ctx.enter_context(nc.sbuf_tensor(name, shape, dt))

        def sem(name):
            s = ctx.enter_context(nc.semaphore(name))
            sems.append(s)
            return s

        sems = []
        rows = sb("gc_rows", [P, 2 * RING, D])
        hot = sb("gc_hot", [P, RING, 2, P])
        dist = sb("gc_dist", [P, 2, 2, P])
        idx = sb("gc_idx", [P, 2, TILES], I32)
        place = sb("gc_place", [P, 2, TILES])
        idx_in = [sem(f"gc_idx_in{b}") for b in range(2)]
        place_in = [sem(f"gc_place_in{b}") for b in range(2)]
        landed = g.landed
        dist_ready, hot_ready, summed, added = sem("gc_dist_ready"), sem("gc_hot_ready"), sem("gc_summed"), sem("gc_added")

        with nc.Block() as block:

            @block.sync
            def _(sp):
                def load_block(i, b):
                    blk = 2 * i + b
                    need(sp, summed, BLOCK * (blk - 1))
                    need(sp, hot_ready, BLOCK * (blk - 1))
                    sp.dma_start(idx[:, b, :], g.idx_d[0, bass.ds(blk, 1)].rearrange("b p t -> (b p) t")).then_inc(idx_in[b], 16)
                    sp.dma_start(place[:, b, :],
                                 g.rec_d[bass.ds(blk, 1), :, REC_PLACE:REC].rearrange("b p t -> (b p) t")).then_inc(place_in[b], 16)

                load_block(0, 0)
                load_block(0, 1)
                with sp.Fori(1, ROUNDS) as i:
                    load_block(i, 0)
                    load_block(i, 1)

            @block.gpsimd
            def _(pool):
                def gather(i):
                    for k in range(RING):
                        b, u = divmod(k, BLOCK)
                        if u == 0:
                            need_apart(pool, idx_in[b], 16 * i + 16)
                        need_apart(pool, summed, RING * i + k - RING + 1)
                        for j in range(2):
                            nc.gpsimd.indirect_dma_start(
                                rows[:, 2 * k + j, :], None, g.xs_d,
                                bass.IndirectOffsetOnAxis(idx[:, b, 2 * u + j:2 * u + j + 1], 0)).then_inc(landed[k], 16)

                gather(0)
                with pool.Fori(1, ROUNDS) as i:
                    gather(i)

            @block.scalar
            def _(act):
                def one_hots(i):
                    for k in range(RING):
                        b, u = divmod(k, BLOCK)
                        n = RING * i + k
                        if u == 0:
                            need(act, place_in[b], 16 * i + 16)
                        for j in range(2):
                            d = act.activation(dist[:, k % 2, j, :], g.iota[:], ACT.Abs,
                                               bias=place[:, b, 2 * u + j:2 * u + j + 1])
                        d.then_inc(dist_ready, 1)
                        need(act, summed, n - RING + 1)
                        act.wait_ge(dist_ready, n + 1)
                        act.activation(hot[:, k], dist[:, k % 2], ACT.Relu, bias=1.0, scale=-1.0).then_inc(hot_ready, 1)

                one_hots(0)
                with act.Fori(1, ROUNDS) as i:
                    one_hots(i)

            @block.tensor
            def _(t):
                def sums(i):
                    for k in range(RING):
                        n = RING * i + k
                        t.wait_ge(hot_ready, n + 1)
                        t.wait_ge(landed[k], 32 * i + 32)
                        need(t, added, n - 1)
                        for j in range(2):
                            mm = t.matmul(g.ps[:, k % 2, 0:D], hot[:, k, j, :], rows[:, 2 * k + j, :],
                                          start=j == 0, stop=j == 1)
                        mm.then_inc(summed, 1)

                sums(0)
                with t.Fori(1, ROUNDS) as i:
                    sums(i)

            @block.vector
            def _(v):
                def add(i):
                    windows = load_words(nc, g.window_rows[0:1, 0], DVE_ENGINE, RING * i, RING)
                    for k in range(RING):
                        n = RING * i + k
                        at = g.sums[:, bass.ds(windows[k] * UROW, D)]
                        keep = g.keep[:, bass.ds(n, 1)]
                        v.wait_ge(summed, n + 1)
                        need(v, added, n)
                        v.scalar_tensor_tensor(out=at, in0=at, scalar=keep, in1=g.ps[:, k % 2, 0:D],
                                               op0=ALU.mult, op1=ALU.add).then_inc(added, 1)

                add(0)
                with v.Fori(1, ROUNDS) as i:
                    add(i)

        end_phase(nc, sems)


def scale_nodes(nc, g):
    with ExitStack() as ctx:
        x = ctx.enter_context(nc.sbuf_tensor("sn_x", [P, 2, D], F32))
        xs = ctx.enter_context(nc.sbuf_tensor("sn_xs", [P, 2, D], F32))
        loaded = [ctx.enter_context(nc.semaphore(f"sn_loaded{b}")) for b in range(2)]
        stored = [ctx.enter_context(nc.semaphore(f"sn_stored{b}")) for b in range(2)]
        scaled = ctx.enter_context(nc.semaphore("sn_scaled"))
        TURNS = WINDOWS // 2
        with nc.Block() as block:

            @block.sync
            def _(sp):
                def load(i):
                    for b in range(2):
                        need(sp, scaled, 2 * i + b - 1)
                        sp.dma_start(x[:, b, :], g.x_d[bass.ds(P * (2 * i + b), P), :]).then_inc(loaded[b], 16)

                load(0)
                with sp.Fori(1, TURNS) as i:
                    load(i)

            @block.vector
            def _(v):
                def scale(i):
                    for b in range(2):
                        factor = g.dis[:, bass.ds(2 * i + b, 1)]
                        v.wait_ge(loaded[b], 16 * i + 16)
                        need(v, stored[b], 16 * i)
                        v.tensor_scalar(xs[:, b, :], x[:, b, :], factor, None,
                                        ALU.mult).then_inc(scaled, 1)

                scale(0)
                with v.Fori(1, TURNS) as i:
                    scale(i)

            @block.scalar
            def _(act):
                def store(i):
                    for b in range(2):
                        act.wait_ge(scaled, 2 * i + b + 1)
                        act.dma_start(g.xs_d[bass.ds(P * (2 * i + b), P), :], xs[:, b, :]).then_inc(stored[b], 16)

                store(0)
                with act.Fori(1, TURNS) as i:
                    store(i)
                for b in range(2):
                    act.wait_ge(stored[b], 16 * TURNS)

        end_phase(nc, loaded + stored + [scaled])


def gcn_nodes(nc, g):
    with ExitStack() as ctx:
        def sb(name, shape, dt=F32):
            return ctx.enter_context(nc.sbuf_tensor(name, shape, dt))

        def sem(name):
            s = ctx.enter_context(nc.semaphore(name))
            sems.append(s)
            return s

        sems = []
        w = sb("gn_w", [P, 2, D])
        x = sb("gn_x", [P, 2, D])
        a = sb("gn_a", [P, 2, D])
        at = sb("gn_at", [P, 2, 2, P])
        y = sb("gn_y", [P, 2, D])
        stat = sb("gn_stat", [P, 2, 6])
        mom = sb("gn_mom", [P, 2, 2])
        rstd = sb("gn_rstd", [P, 2, 1])
        var = sb("gn_var", [P, 1])
        bits = sb("gn_bits", [P, 1], I32)
        half = sb("gn_half", [P, 1])
        out = sb("gn_out", [P, 2, D])
        w_in = sem("gn_w_in")
        x_in = [sem(f"gn_x_in{b}") for b in range(2)]
        stored = [sem(f"gn_stored{b}") for b in range(2)]
        scaled, turned, copied, mixed, vec, normed = (
            sem("gn_scaled"), sem("gn_turned"), sem("gn_copied"), sem("gn_mixed"), sem("gn_vec"), sem("gn_normed"))
        TURNS = WINDOWS // 2
        ps = g.ps
        with nc.Block() as block:

            @block.sync
            def _(sp):
                sp.dma_start(w[:], g.gcn_w.rearrange("(c k) n -> k c n", c=2)).then_inc(w_in, 16)

                def load(i):
                    for b in range(2):
                        need(sp, normed, 2 * i + b - 1)
                        sp.dma_start(x[:, b, :], g.x_d[bass.ds(P * (2 * i + b), P), :]).then_inc(x_in[b], 16)

                load(0)
                with sp.Fori(1, TURNS) as i:
                    load(i)

            @block.tensor
            def _(t):
                t.wait_ge(w_in, 16)

                def mix(i):
                    for b in range(2):
                        n = 2 * i + b
                        t.wait_ge(scaled, n + 1)
                        need(t, copied, n - 1)
                        for c in range(2):
                            tr = t.transpose(ps[:, b, c * P:(c + 1) * P], a[:, b, c * P:(c + 1) * P], g.ident[:])
                        tr.then_inc(turned, 1)
                        t.wait_ge(copied, n + 1)
                        need(t, normed, n - 1)
                        for c in range(2):
                            mm = t.matmul(ps[:, 2 + b, 0:D], at[:, b, c, :], w[:, c, :], start=c == 0, stop=c == 1)
                        mm.then_inc(mixed, 1)

                mix(0)
                with t.Fori(1, TURNS) as i:
                    mix(i)

            @block.scalar
            def _(act):
                def copy(i):
                    for b in range(2):
                        n = 2 * i + b
                        act.wait_ge(turned, n + 1)
                        need(act, mixed, n - 1)
                        act.copy(at[:, b], ps[:, b, 0:D].rearrange("p (c n) -> p c n", c=2)).then_inc(copied, 1)
                        if not (isinstance(n, int) and n == 0):
                            store(n - 1, 1 - b)

                def store(n, b):
                    act.wait_ge(normed, n + 1)
                    for dram in (g.x_d, g.x1_d):
                        act.dma_start(dram[bass.ds(P * n, P), :], out[:, b, :]).then_inc(stored[b], 16)

                copy(0)
                with act.Fori(1, TURNS) as i:
                    copy(i)
                store(WINDOWS - 1, 1)
                for b in range(2):
                    act.wait_ge(stored[b], 32 * TURNS)

            @block.vector
            def _(v):
                def scale(n, b):
                    sums, factor = g.sums[:, bass.ds(UROW * n, D)], g.dis[:, bass.ds(n, 1)]
                    need(v, turned, n - 1)
                    v.tensor_scalar(a[:, b, :], sums, factor, None,
                                    ALU.mult).then_inc(scaled, 1)

                def norm(i, b):
                    n = 2 * i + b
                    v.wait_ge(mixed, n + 1)
                    v.wait_ge(x_in[b], 16 * i + 16)
                    count = (4 + RSQRT_SIGNALS) * n
                    v.tensor_tensor(y[:, b, :], ps[:, 2 + b, 0:D], x[:, b, :], ALU.add).then_inc(vec, 1)
                    v.wait_ge(vec, count + 1)
                    v.bn_stats(stat[:, b, :], y[:, b, :]).then_inc(vec, 1)
                    need_apart(v, vec, count + 2)
                    v.bn_aggr(mom[:, b, :], stat[:, b, :]).then_inc(vec, 1)
                    v.wait_ge(vec, count + 3)
                    v.tensor_scalar(var[:], mom[:, b, 1:2], EPS, None, ALU.add).then_inc(vec, 1)
                    v.wait_ge(vec, count + 4)
                    reciprocal_sqrt(v, var[:], rstd[:, b, :], bits[:], half[:], vec, count + 4)
                    need(v, stored[b], 32 * i)
                    v.tensor_scalar(out[:, b, :], y[:, b, :], mom[:, b, 0:1], rstd[:, b, :], ALU.subtract,
                                    ALU.mult).then_inc(normed, 1)

                def turn(i, more=True):
                    scale(2 * i + 1, 1)
                    norm(i, 0)
                    if more:
                        scale(2 * i + 2, 0)
                    norm(i, 1)

                scale(0, 0)
                turn(0)
                with v.Fori(1, TURNS - 1) as i:
                    turn(i)
                turn(TURNS - 1, more=False)

        end_phase(nc, sems)


def project(nc, g, layer):
    with ExitStack() as ctx:
        def sb(name, shape, dt=F32):
            return ctx.enter_context(nc.sbuf_tensor(name, shape, dt))

        def sem(name):
            s = ctx.enter_context(nc.semaphore(name))
            sems.append(s)
            return s

        sems = []
        wk = sb("pj_wk", [P, HEADS, HD])
        wkt = sb("pj_wkt", [HD, HEADS, P])
        we = sb("pj_we", [HD, EDGE_TYPES, HEADS, HD])
        mu = sb("pj_mu", [P, HEADS, EDGE_TYPES])
        w = sb("pj_w", [P, HEADS, PROJ, HD])
        x = sb("pj_x", [P, 2, D])
        xm = sb("pj_xm", [P, 2, HEADS, NODE_TYPES, HD])
        xmt = sb("pj_xmt", [P, 2, HEADS, P])
        ks = sb("pj_k", [P, 2, EDGE_TYPES, HEADS, HD])
        vs = sb("pj_v", [P, 2, HEADS, HD])
        w_in, kt_turned, kt_copied, w_mixed, mu_scaled, w_ready = (
            sem("pj_w_in"), sem("pj_kt_turned"), sem("pj_kt_copied"), sem("pj_w_mixed"), sem("pj_mu_scaled"),
            sem("pj_w_ready"))
        x_in = [sem(f"pj_x_in{b}") for b in range(2)]
        stored = [sem(f"pj_stored{b}") for b in range(2)]
        masked, turned, copied, mixed, out_v, out_k, out_q = (
            sem("pj_masked"), sem("pj_turned"), sem("pj_copied"), sem("pj_mixed"), sem("pj_out_v"), sem("pj_out_k"),
            sem("pj_out_q"))
        TURNS = WINDOWS // 2
        ps = g.ps
        BANK_HEADS = (range(0, 3), range(3, 6), range(6, 8))
        WIDTH = PROJ * HD

        def bank(b, k):
            return ps[:, 2 + 3 * b + k, 0:len(BANK_HEADS[k]) * WIDTH].rearrange("p (h o e) -> p h o e", o=PROJ, e=HD)

        with nc.Block() as block:

            @block.sync
            def _(sp):
                for t in range(NODE_TYPES):
                    rows = slice(t * HD, (t + 1) * HD)
                    for dram, dest in ((g.w_k, wk[rows, :, :]), (g.w_q, w[rows, :, 0, :]), (g.w_v, w[rows, :, 1, :])):
                        sp.dma_start(dest, dram[bass.ds(layer, 1), t].rearrange("a h d e -> (a d) h e")).then_inc(w_in, 16)
                sp.dma_start(we[:], g.w_e[bass.ds(layer, 1)].rearrange("a t h m e -> (a m) t h e")).then_inc(w_in, 16)
                sp.dma_start(mu[:].rearrange("p h t -> p (h t)"),
                             g.mu[bass.ds(layer, 1)].rearrange("a h t -> a (h t)")
                             .to_broadcast([P, HEADS * EDGE_TYPES])).then_inc(w_in, 16)

                def store(i):
                    for b in range(2):
                        n = 2 * i + b
                        sp.wait_ge(out_k, n + 1)
                        rows = g.tab_d[:, bass.ds(P * n, P), :].rearrange("t p c -> p t c")
                        sp.dma_start(rows[:, :, 0:D], ks[:, b].rearrange("p t h e -> p t (h e)")).then_inc(stored[b], 16)
                        sp.dma_start(rows[:, :, D:ROW],
                                     vs[:, b].rearrange("p h e -> p (h e)")[:, None, :]
                                     .to_broadcast([P, EDGE_TYPES, D])).then_inc(stored[b], 16)

                store(0)
                with sp.Fori(1, TURNS) as i:
                    store(i)
                for b in range(2):
                    sp.wait_ge(stored[b], 32 * TURNS)

            @block.tensor
            def _(t):
                t.wait_ge(w_in, 16 * 14)
                for h in range(HEADS):
                    tr = t.transpose(ps[0:HD, h // 4, (h % 4) * P:(h % 4 + 1) * P], wk[:, h, :], g.ident[:])
                tr.then_inc(kt_turned, 1)
                t.wait_ge(kt_copied, 1)
                for h in range(HEADS):
                    mm = t.matmul(ps[:, 2 + h // 4, (h % 4) * EDGE_TYPES * HD:(h % 4 + 1) * EDGE_TYPES * HD],
                                  wkt[:, h, :], we[:, :, h, :], start=True, stop=True)
                mm.then_inc(w_mixed, 1)

                def turn(n, b):
                    t.wait_ge(masked, n + 1)
                    need(t, copied, n)
                    for h in range(HEADS):
                        tr = t.transpose(ps[:, h // 4, (h % 4) * P:(h % 4 + 1) * P],
                                         xm[:, b, h].rearrange("p t d -> p (t d)"), g.ident[:])
                    tr.then_inc(turned, 1)

                def mix(n, b):
                    t.wait_ge(copied, n + 1)
                    need(t, out_v, 3 * (n - 1))
                    need(t, out_k, n - 1)
                    for k, heads in enumerate(BANK_HEADS):
                        for h in heads:
                            mm = t.matmul(bank(b, k)[:, h - heads[0]], xmt[:, b, h, :], w[:, h], start=True, stop=True)
                    mm.then_inc(mixed, 1)

                turn(0, 0)
                t.wait_ge(w_ready, 1)
                turn(1, 1)
                mix(0, 0)
                with t.Fori(1, TURNS) as i:
                    turn(2 * i, 0)
                    mix(2 * i - 1, 1)
                    turn(2 * i + 1, 1)
                    mix(2 * i, 0)
                mix(WINDOWS - 1, 1)

            @block.scalar
            def _(act):
                def load(i, b):
                    need(act, masked, 2 * i + b - 1)
                    act.dma_start(x[:, b, :], g.x_d[bass.ds(P * (2 * i + b), P), :]).then_inc(x_in[b], 16)

                load(0, 0)
                load(0, 1)
                act.wait_ge(kt_turned, 1)
                act.copy(wkt[:].rearrange("p (b h) n -> p b (h n)", b=2), ps[0:HD, 0:2, :]).then_inc(kt_copied, 1)

                def copy(n, b):
                    act.wait_ge(turned, n + 1)
                    need(act, mixed, n - 1)
                    act.copy(xmt[:, b].rearrange("p (k h) n -> p k (h n)", k=2), ps[:, 0:2, :]).then_inc(copied, 1)

                def out(i, b):
                    n = 2 * i + b
                    act.wait_ge(mixed, n + 1)
                    need(act, stored[b], 32 * i)
                    for k, heads in enumerate(BANK_HEADS):
                        act.copy(vs[:, b, heads[0]:heads[-1] + 1, :], bank(b, k)[:, :, 1, :]).then_inc(out_v, 1)

                copy(0, 0)
                load(1, 0)
                copy(1, 1)
                load(1, 1)
                out(0, 0)

                def turn(i, more=True):
                    copy(2 * i, 0)
                    if more:
                        load(i + 1, 0)
                    out(i - 1, 1)
                    copy(2 * i + 1, 1)
                    if more:
                        load(i + 1, 1)
                    out(i, 0)

                with act.Fori(1, TURNS - 1) as i:
                    turn(i)
                turn(TURNS - 1, more=False)
                out(TURNS - 1, 1)

            @block.gpsimd
            def _(pool):
                def mask(i, b):
                    n = 2 * i + b
                    shape = [P, HEADS, NODE_TYPES, HD]
                    types = g.type_hot[:, bass.ds(n, 1), :][:, :, :, None].to_broadcast(shape)
                    pool.wait_ge(x_in[b], 16 * i + 16)
                    need(pool, turned, n - 1)
                    nc.gpsimd.tensor_tensor(xm[:, b],
                                    x[:, b, :].rearrange("p (h d) -> p h d", h=HEADS)[:, :, None, :].to_broadcast(shape),
                                    types, ALU.mult).then_inc(masked, 1)

                mask(0, 0)
                mask(0, 1)
                with pool.Fori(1, TURNS) as i:
                    mask(i, 0)
                    mask(i, 1)

            @block.vector
            def _(v):
                v.wait_ge(w_in, 16 * 14)
                v.tensor_scalar(mu[:], mu[:], float(HD) ** -0.5, None, ALU.mult).then_inc(mu_scaled, 1)

                def out(i, b):
                    n = 2 * i + b
                    need(v, stored[b], 32 * i)
                    for k, heads in enumerate(BANK_HEADS):
                        q_row = g.sums[:, bass.ds(UROW * (n + 1) + heads[0] * HD, len(heads) * HD)]
                        v.wait_ge(out_v, 3 * n + k + 1)
                        v.tensor_copy(ks[:, b, :, heads[0]:heads[-1] + 1, :].rearrange("p t h e -> p h t e"),
                                      bank(b, k)[:, :, 2:PROJ, :])
                        d = v.tensor_copy(q_row.rearrange("p (h e) -> p h e", e=HD), bank(b, k)[:, :, 0, :])
                    d.then_inc(out_k, 1)

                v.wait_ge(w_mixed, 1)
                v.wait_ge(mu_scaled, 1)
                for half in range(2):
                    shape = [P, 4, EDGE_TYPES, HD]
                    d = v.tensor_tensor(w[:, 4 * half:4 * half + 4, 2:PROJ, :],
                                        ps[:, 2 + half, 0:4 * EDGE_TYPES * HD].rearrange("p (h t e) -> p h t e", h=4, t=EDGE_TYPES),
                                        mu[:, 4 * half:4 * half + 4, :, None].to_broadcast(shape), ALU.mult)
                d.then_inc(w_ready, 1)
                with v.Fori(1, TURNS) as i:
                    out(i - 1, 0)
                    out(i - 1, 1)
                out(TURNS - 1, 0)
                out(TURNS - 1, 1)

        end_phase(nc, sems)


LAG_COPY = 1
LAG_SCORE = 2
LAG_WEIGH = 13
LAG_SUM = 14
LAG_ADD = 15
SOFT_TURN, SOFT_CROSS, SOFT_OUT, SOFT_RESCALE = 2, 3, 4, 7


def attention_edges(nc, g, layer):
    with ExitStack() as ctx:
        def sb(name, shape, dt=F32):
            return ctx.enter_context(nc.sbuf_tensor(name, shape, dt))

        def sem(name):
            s = ctx.enter_context(nc.semaphore(name))
            sems.append(s)
            return s

        sems = []
        kv = sb("at_kv", [P, 2 * RING, SLOT])
        hot = sb("at_hot", [P, RING, 2, P])
        hot_t = sb("at_hot_t", [P, 2, 2, P])
        dist = sb("at_dist", [P, 2, 2, P])
        idx = sb("at_idx", [P, 2, TILES], I32)
        rec = sb("at_rec", [P, 2, REC])
        score = sb("at_score", [P, 2, TILES, HEADS])
        floor = sb("at_floor", [P, P])
        run = sb("at_run", [P, P])
        top = sb("at_top", [P, P])
        ends = sb("at_ends", [P, CROSS])
        seen = sb("at_seen", [P, 2, CROSS])
        ends_max = sb("at_ends_max", [P, 2, 2])
        fall = sb("at_fall", [P, 1])
        fall_row = sb("at_fall_row", [P, P])
        top_first = sb("at_top_first", [P, P])
        top_all = sb("at_top_all", [P, P])
        less = sb("at_less", [P, P])
        fade = sb("at_fade", [P, 2, HEADS])
        idx_in = [sem(f"at_idx_in{b}") for b in range(2)]
        rec_in = [sem(f"at_rec_in{b}") for b in range(2)]
        landed = g.landed
        before = PASS_LANDED * (layer + 1)
        (dist_ready, hot_ready, turned, copied, q_ready, multiplied, scored, weighed, summed, added) = (
            sem("at_dist_ready"), sem("at_hot_ready"), sem("at_turned"), sem("at_copied"), sem("at_q_ready"),
            sem("at_multiplied"), sem("at_scored"), sem("at_weighed"), sem("at_summed"), sem("at_added"))
        (scores_turned, soft, ends_ready, crossed, less_ready, less_turned, faded, weights_ready, rescaled) = (
            sem("at_scores_turned"), sem("at_soft"), sem("at_ends_ready"), sem("at_crossed"),
            sem("at_less_ready"), sem("at_less_turned"), sem("at_faded"),
            sem("at_weights_ready"), sem("at_rescaled"))
        ps = g.ps
        TURN_BANK, Q_BANK, SUM_BANK, SOFT_BANK = 0, 2, 4, 6
        SCORES_T, ENDS_AT, FADE_AT, LESS_T = slice(0, P), slice(P, P + CROSS), slice(176, 176 + HEADS), slice(2 * P, 3 * P)

        def steps(i, emit):
            for k in range(RING):
                def at(lag, k=k):
                    n = RING * i + (k - lag)
                    if isinstance(n, int) and not 0 <= n < PAIRS:
                        return None
                    return n, (k - lag) % RING, i + (k - lag) // RING
                emit(k, at)

        def soft_block(i, k, stage):
            if k % BLOCK != stage:
                return None
            b = 2 * i + k // BLOCK - 1
            if isinstance(b, int) and not 0 <= b < BLOCKS:
                return None
            return b, (k // BLOCK - 1) % 2

        with nc.Block() as block:

            @block.sync
            def _(sp):
                def load_block(i, b):
                    blk = 2 * i + b
                    need(sp, less_ready, blk - 1)
                    sp.dma_start(idx[:, b, :], g.idx_d[1, bass.ds(blk, 1)].rearrange("b p t -> (b p) t")).then_inc(idx_in[b], 16)
                    sp.dma_start(rec[:, b, :], g.rec_d[bass.ds(blk, 1)].rearrange("b p r -> (b p) r")).then_inc(rec_in[b], 16)

                load_block(0, 0)
                load_block(0, 1)
                with sp.Fori(1, ROUNDS) as i:
                    load_block(i, 0)
                    load_block(i, 1)

            @block.gpsimd
            def _(pool):
                def gather(i):
                    for k in range(RING):
                        b, u = divmod(k, BLOCK)
                        if u == 0:
                            need_apart(pool, idx_in[b], 16 * i + 16)
                        need_apart(pool, summed, RING * i + k - RING + 1)
                        for j in range(2):
                            nc.gpsimd.indirect_dma_start(
                                kv[:, 2 * k + j, 0:ROW], None, g.tab_d.rearrange("t n c -> (t n) c"),
                                bass.IndirectOffsetOnAxis(idx[:, b, 2 * u + j:2 * u + j + 1], 0)).then_inc(landed[k], 16)

                gather(0)
                with pool.Fori(1, ROUNDS) as i:
                    gather(i)

            @block.scalar
            def _(act):
                def emit(k, at, i):
                    if now := at(0):
                        n, slot, turn = now
                        b, u = divmod(slot, BLOCK)
                        if u == 0:
                            act.wait_ge(rec_in[b], 16 * turn + 16)
                        for j in range(2):
                            d = act.activation(dist[:, slot % 2, j, :], g.iota[:], ACT.Abs,
                                               bias=rec[:, b, REC_PLACE + 2 * u + j:REC_PLACE + 2 * u + j + 1])
                        d.then_inc(dist_ready, 1)
                    if now := at(LAG_COPY):
                        n, slot, turn = now
                        act.wait_ge(turned, n + 1)
                        need(act, q_ready, n - 1)
                        act.copy(hot_t[:, slot % 2].rearrange("p j e -> p (j e)"),
                                 ps[:, TURN_BANK + slot % 2, 0:GROUP]).then_inc(copied, 1)
                    if now := at(0):
                        n, slot, turn = now
                        need(act, summed, n - RING + 1)
                        act.wait_ge(dist_ready, n + 1)
                        act.activation(hot[:, slot], dist[:, slot % 2], ACT.Relu, bias=1.0, scale=-1.0).then_inc(hot_ready, 1)
                    if blk := soft_block(i, k, SOFT_OUT):
                        b, par = blk
                        act.wait_ge(less_turned, b + 1)
                        need(act, rescaled, b - 1)
                        act.activation(fade[:, par, :], ps[:, SOFT_BANK + par, FADE_AT], ACT.Exp).then_inc(faded, 1)
                        act.activation(kv[:, TILES * par:TILES * (par + 1), ROW:SLOT],
                                       ps[:, SOFT_BANK + par, LESS_T].rearrange("p (t h) -> p t h", h=HEADS),
                                       ACT.Exp).then_inc(weights_ready, 1)

                def turn(i):
                    steps(i, lambda k, at: emit(k, at, i))

                turn(0)
                with act.Fori(1, ROUNDS) as i:
                    turn(i)
                turn(ROUNDS)

            @block.tensor
            def _(t):
                def emit(k, at, i, windows):
                    if now := at(0):
                        n, slot, turn = now
                        t.wait_ge(hot_ready, n + 1)
                        need(t, copied, n - 1)
                        for j in range(2):
                            tr = t.transpose(ps[:, TURN_BANK + slot % 2, j * P:(j + 1) * P], hot[:, slot, j, :], g.ident[:])
                        tr.then_inc(turned, 1)
                    if blk := soft_block(i, k, SOFT_TURN):
                        b, par = blk
                        t.wait_ge(scored, BLOCK * (b + 1))
                        need(t, weights_ready, b - 1)
                        t.transpose(ps[:, SOFT_BANK + par, SCORES_T], score[:, par].rearrange("p t h -> p (t h)"),
                                    g.ident[:]).then_inc(scores_turned, 1)
                    if blk := soft_block(i, k, SOFT_CROSS):
                        b, par = blk
                        t.wait_ge(ends_ready, b + 1)
                        t.matmul(ps[:, SOFT_BANK + par, ENDS_AT], g.same_head[:], ends[:], start=True, stop=True).then_inc(crossed, 1)
                    if blk := soft_block(i, k, SOFT_OUT):
                        b, par = blk
                        t.wait_ge(less_ready, b + 1)
                        t.matmul(ps[:, SOFT_BANK + par, FADE_AT], fall_row[:], g.ident[:, 0:HEADS], start=True, stop=True)
                        t.transpose(ps[:, SOFT_BANK + par, LESS_T], less[:], g.ident[:]).then_inc(less_turned, 1)
                    if now := at(LAG_SUM):
                        n, slot, turn = now
                        t.wait_ge(weighed, n + 1)
                        need(t, added, n - 1)
                        for j in range(2):
                            mm = t.matmul(ps[:, SUM_BANK + slot % 2, 0:UROW], hot[:, slot, j, :], kv[:, 2 * slot + j, D:SLOT],
                                          start=j == 0, stop=j == 1)
                        mm.then_inc(summed, 1)
                    if k == 0:
                        windows.extend(load_words(nc, g.window_rows[0:1, g.shifts.index(LAG_COPY)], PE_ENGINE, RING * i, RING))
                    if now := at(LAG_COPY):
                        n, slot, turn = now
                        q_rows = g.sums[:, bass.ds(windows[k] * UROW + UROW, D)]
                        t.wait_ge(copied, n + 1)
                        need(t, multiplied, n - 1)
                        for j in range(2):
                            mm = t.matmul(ps[:, Q_BANK + slot % 2, j * D:(j + 1) * D], hot_t[:, slot % 2, j, :], q_rows,
                                          start=True, stop=True)
                        mm.then_inc(q_ready, 1)

                def turn(i):
                    windows = []
                    steps(i, lambda k, at: emit(k, at, i, windows))

                turn(0)
                with t.Fori(1, ROUNDS) as i:
                    turn(i)
                turn(ROUNDS)

            @block.vector
            def _(v):
                def emit(k, at, i, windows):
                    score_now, weigh_now, add_now = at(LAG_SCORE), at(LAG_WEIGH), at(LAG_ADD)
                    maxima, across = soft_block(i, k, SOFT_TURN), soft_block(i, k, SOFT_CROSS)
                    if score_now:
                        n, slot, turn = score_now
                        v.wait_ge(q_ready, n + 1)
                        v.wait_ge(landed[slot], before + 32 * turn + 32)
                        keys = kv[:, 2 * slot:2 * slot + 2, 0:D]
                        v.tensor_tensor(keys, ps[:, Q_BANK + slot % 2, :].rearrange("p (j c) -> p j c", j=2), keys,
                                        ALU.mult).then_inc(multiplied, 1)
                    if across:
                        b, par = across
                        v.wait_ge(crossed, b + 1)
                        need(v, less_turned, b)
                        shape = [P, 2, CROSS]
                        v.tensor_tensor(seen[:], ps[:, SOFT_BANK + par, ENDS_AT][:, None, :].to_broadcast(shape),
                                        rec[:, par, REC_CROSS:REC_CARRY].rearrange("p (k c) -> p k c", k=2),
                                        ALU.add).then_inc(soft, 1)
                    if weigh_now:
                        n, slot, turn = weigh_now
                        if slot % BLOCK == 0:
                            v.wait_ge(weights_ready, 2 * turn + slot // BLOCK + 1)
                        shape = [P, 2, HEADS, HD]
                        values = kv[:, 2 * slot:2 * slot + 2, D:ROW].rearrange("p j (h e) -> p j h e", h=HEADS)
                        v.tensor_tensor(values, values,
                                        kv[:, 2 * slot:2 * slot + 2, ROW:SLOT][:, :, :, None].to_broadcast(shape),
                                        ALU.mult).then_inc(weighed, 1)
                    if maxima:
                        b, par = maxima
                        v.wait_ge(scores_turned, b + 1)
                        v.wait_ge(rec_in[par], 8 * (b - par) + 16)
                        need(v, crossed, b)
                        v.tensor_tensor(ends[:, CROSS - 1:CROSS], g.tile_hot[:, TILES - 1:TILES],
                                        ends_max[:, 1 - par, 1:2], ALU.mult)
                        v.tensor_scalar(floor[:], ps[:, SOFT_BANK + par, SCORES_T], FLOOR, None, ALU.max).then_inc(soft, 1)
                    if across:
                        b, par = across
                        v.wait_ge(soft, 8 * b + 5)
                        v.tensor_reduce(ends_max[:, par, :], seen[:], AX.X, ALU.max).then_inc(soft, 1)
                    if score_now:
                        n, slot, turn = score_now
                        par, u = divmod(slot, BLOCK)
                        v.wait_ge(multiplied, n + 1)
                        if u == 0:
                            need(v, scores_turned, 2 * turn + par - 1)
                        v.tensor_reduce(score[:, par, 2 * u:2 * u + 2, :],
                                        kv[:, 2 * slot:2 * slot + 2, 0:D].rearrange("p j (h e) -> p j h e", h=HEADS),
                                        AX.X, ALU.add).then_inc(scored, 1)
                    if k == 0:
                        windows.extend(load_words(nc, g.window_rows[0:1, g.shifts.index(LAG_ADD)], DVE_ENGINE, RING * i, RING))
                    if maxima:
                        b, par = maxima
                        v.wait_ge(soft, 8 * b + 2)
                        v.tensor_tensor_scan(run[:], rec[:, par, REC_PEN:REC_PEN + P], floor[:], 0.0, ALU.add,
                                             ALU.max).then_inc(soft, 1)
                    if across:
                        b, par = across
                        v.wait_ge(soft, 8 * b + 6)
                        v.tensor_tensor(fall[:], ps[:, SOFT_BANK + par, P + CROSS - 1:P + CROSS], ends_max[:, par, 0:1],
                                        ALU.subtract).then_inc(soft, 1)
                        v.scalar_tensor_tensor(out=top_first[:], in0=rec[:, par, REC_FIRST:REC_FIRST + P],
                                               scalar=ends_max[:, par, 0:1], in1=top[:], op0=ALU.add,
                                               op1=ALU.max).then_inc(soft, 1)
                    if blk := soft_block(i, k, SOFT_RESCALE):
                        b, par = blk
                        values = g.sums[:, bass.ds(windows[k - 1] * UROW, D)].rearrange("p (h e) -> p h e", h=HEADS)
                        weights = g.sums[:, bass.ds(windows[k - 1] * UROW + D, HEADS)]
                        v.wait_ge(faded, b + 1)
                        need(v, added, BLOCK * b)
                        v.tensor_tensor(values, values, fade[:, par, :, None].to_broadcast([P, HEADS, HD]), ALU.mult)
                        v.tensor_tensor(weights, weights, fade[:, par, :], ALU.mult).then_inc(rescaled, 1)
                    if add_now:
                        n, slot, turn = add_now
                        rows = g.sums[:, bass.ds(windows[k] * UROW, UROW)]
                        keep = g.keep[:, bass.ds(n, 1)]
                        v.wait_ge(summed, n + 1)
                        need(v, added, n)
                        if slot % BLOCK == 0:
                            v.wait_ge(rescaled, 2 * turn + slot // BLOCK + 1)
                        v.scalar_tensor_tensor(out=rows, in0=rows, scalar=keep,
                                               in1=ps[:, SUM_BANK + slot % 2, 0:UROW], op0=ALU.mult, op1=ALU.add).then_inc(added, 1)
                    if maxima:
                        b, par = maxima
                        v.wait_ge(soft, 8 * b + 3)
                        v.tensor_tensor_scan(top[:, ::-1], rec[:, par, REC_PEN + P:REC_PEN:-1], run[:, ::-1], 0.0,
                                             ALU.add, ALU.max).then_inc(soft, 1)
                        v.wait_ge(soft, 8 * b + 4)
                        shape = [P, 2, TILES]
                        v.tensor_tensor(ends[:, 0:2 * TILES].rearrange("p (k t) -> p k t", k=2),
                                        g.tile_hot[:, None, :].to_broadcast(shape),
                                        top[:, ::P - 1][:, :, None].to_broadcast(shape), ALU.mult).then_inc(ends_ready, 1)
                    if across:
                        b, par = across
                        v.wait_ge(soft, 8 * b + 7)
                        v.tensor_scalar(fall_row[:], g.iota[:], rec[:, par, REC_CARRY:REC_CARRY + 1], fall[:],
                                        ALU.is_equal, ALU.mult)
                        v.wait_ge(soft, 8 * b + 8)
                        v.scalar_tensor_tensor(out=top_all[:], in0=rec[:, par, REC_LAST:REC_LAST + P],
                                               scalar=ends_max[:, par, 1:2], in1=top_first[:], op0=ALU.add,
                                               op1=ALU.max).then_inc(soft, 1)
                        v.wait_ge(soft, 8 * b + 9)
                        v.tensor_tensor(less[:], ps[:, SOFT_BANK + par, SCORES_T], top_all[:], ALU.subtract).then_inc(less_ready, 1)

                def turn(i):
                    windows = []
                    steps(i, lambda k, at: emit(k, at, i, windows))

                v.memset(ends_max[:], 0.0).then_inc(soft, 1)
                v.wait_ge(soft, 1)
                turn(0)
                with v.Fori(1, ROUNDS) as i:
                    turn(i)
                turn(ROUNDS)

        end_phase(nc, sems)


class NormTiles:

    def __init__(self, sb, name):
        self.stat = sb(name + "_stat", [P, 2, 6])
        self.mom = sb(name + "_mom", [P, 2, 2])
        self.var = sb(name + "_var", [P, 2])
        self.rstd = sb(name + "_rstd", [P, 2])
        self.bits = sb(name + "_bits", [P, 2], I32)
        self.half = sb(name + "_half", [P, 2])


NORM_SIGNALS = 4 + RSQRT_SIGNALS


def layer_norm(v, y, s, out, done, count):
    for a in range(2):
        d = v.bn_stats(s.stat[:, a, :], y[:, a, :])
    d.then_inc(done, 1)
    need_apart(v, done, count + 1)
    for a in range(2):
        d = v.bn_aggr(s.mom[:, a, :], s.stat[:, a, :])
    d.then_inc(done, 1)
    v.wait_ge(done, count + 2)
    v.tensor_scalar(s.var[:], s.mom[:, :, 1], EPS, None, ALU.add).then_inc(done, 1)
    v.wait_ge(done, count + 3)
    reciprocal_sqrt(v, s.var[:], s.rstd[:], s.bits[:], s.half[:], done, count + 3)
    for a in range(2):
        d = v.tensor_scalar(out[:, a, :], y[:, a, :], s.mom[:, a, 0:1], s.rstd[:, a:a + 1], ALU.subtract, ALU.mult)
    d.then_inc(done, 1)
    v.wait_ge(done, count + NORM_SIGNALS)


def both(vector):
    return vector[:, None, :].to_broadcast([P, 2, D])


def attention_nodes(nc, g, layer):
    with ExitStack() as ctx:
        def sb(name, shape, dt=F32):
            return ctx.enter_context(nc.sbuf_tensor(name, shape, dt))

        def sem(name):
            s = ctx.enter_context(nc.semaphore(name))
            sems.append(s)
            return s

        sems = []
        HC = HIDDEN // P
        wo = sb("an_wo", [P, 2, D])
        w1 = sb("an_w1", [P, 2, HIDDEN])
        w2 = sb("an_w2", [P, HC, D])
        b1_row = sb("an_b1_row", [HC, P])
        b1 = sb("an_b1", [P, HC])
        rows = sb("an_rows", [P, 6, D])
        x = sb("an_x", [P, 2, 2, D])
        some = sb("an_some", [P, 2, 2, HEADS])
        part = sb("an_part", [P, 2, 2, HEADS])
        a = sb("an_a", [P, 2, 2, D])
        at = sb("an_at", [P, 2, 2, P])
        xb = sb("an_xb", [P, 2, 2, D])
        y = sb("an_y", [P, 2, D])
        yn = sb("an_yn", [P, 2, D])
        yg = sb("an_yg", [P, 2, D])
        zn = sb("an_zn", [P, 2, D])
        zg = sb("an_zg", [P, 2, D])
        scratch = NormTiles(sb, "an")
        x1 = sb("an_x1", [P, 2, 2, D])
        x1b = sb("an_x1b", [P, 2, 2, D])
        x1t = sb("an_x1t", [P, 2, 2, P])
        ht = sb("an_ht", [P, HC, 2 * P])
        out = sb("an_out", [P, 2, 2, D])
        w_in = sem("an_w_in")
        x_in = [sem(f"an_x_in{b}") for b in range(2)]
        stored = [sem(f"an_stored{b}") for b in range(2)]
        (b1_turned, b1_copied, shared, averaged, a_turned, a_copied, attended, vec1, x1_ready, x1_turned, x1_copied,
         hidden, activated, fed, vec2, normed, x_biased, x1_biased, gained) = (
            sem("an_b1_turned"), sem("an_b1_copied"), sem("an_shared"), sem("an_averaged"), sem("an_a_turned"),
            sem("an_a_copied"), sem("an_attended"), sem("an_vec1"), sem("an_x1_ready"), sem("an_x1_turned"),
            sem("an_x1_copied"), sem("an_hidden"), sem("an_activated"), sem("an_fed"), sem("an_vec2"), sem("an_normed"),
            sem("an_x_biased"), sem("an_x1_biased"), sem("an_gained"))
        STEPS = WINDOWS // 2
        CHAIN1 = 2 + NORM_SIGNALS
        CHAIN2 = 1 + NORM_SIGNALS
        BO, LN1_G, LN1_B, B2, LN2_G, LN2_B = range(6)
        ps = g.ps

        def turns(eng, emit):
            def turn(i):
                for b in range(2):
                    emit(2 * i + b, b, i)

            turn(0)
            turn(1)
            with eng.Fori(2, STEPS // 2) as i:
                turn(i)
            turn(STEPS // 2)
            turn(STEPS // 2 + 1)

        def real(m):
            return not isinstance(m, int) or 0 <= m < STEPS

        with nc.Block() as block:

            @block.sync
            def _(sp):
                sp.dma_start(wo[:], g.wo[bass.ds(layer, 1)].rearrange("a (c k) n -> k (a c) n", c=2)).then_inc(w_in, 16)
                for k, dram in enumerate((g.bo, g.ln1_g, g.ln1_b, g.b2, g.ln2_g, g.ln2_b)):
                    sp.dma_start(rows[:, k, :], dram[bass.ds(layer, 1), :].to_broadcast([P, D])).then_inc(w_in, 16)
                sp.dma_start(b1_row[:], g.b1[bass.ds(layer, 1)].rearrange("a (c k) -> (a c) k", c=HC)).then_inc(w_in, 16)
                sp.dma_start(w1[:], g.w1[bass.ds(layer, 1)].rearrange("a (c k) n -> k (a c) n", c=2)).then_inc(w_in, 16)
                sp.dma_start(w2[:], g.w2[bass.ds(layer, 1)].rearrange("a (c k) n -> k (a c) n", c=HC)).then_inc(w_in, 16)

                def emit(n, b, i):
                    if real(n):
                        need(sp, x_biased, n - 1)
                        sp.dma_start(x[:, b], g.x_d[bass.ds(2 * P * n, 2 * P), :].rearrange("(a p) c -> p a c", a=2)).then_inc(x_in[b], 16)
                    if real(n - 2):
                        sp.wait_ge(normed, n - 1)
                        sp.dma_start(g.x_d[bass.ds(2 * P * (n - 2), 2 * P), :].rearrange("(a p) c -> p a c", a=2),
                                     out[:, b]).then_inc(stored[b], 16)

                turns(sp, emit)
                sp.wait_ge(stored[0], 16 * ((STEPS + 1) // 2))
                sp.wait_ge(stored[1], 16 * (STEPS // 2))

            @block.tensor
            def _(t):
                t.wait_ge(w_in, 16 * 10)
                t.transpose(ps[:, 2, 0:HC], b1_row[:], g.ident[0:HC, 0:HC]).then_inc(b1_turned, 1)
                t.wait_ge(b1_copied, 1)

                def emit(n, b, i):
                    if real(n):
                        t.wait_ge(averaged, n + 1)
                        need(t, a_copied, n)
                        for q in range(4):
                            tr = t.transpose(ps[:, 0, q * P:(q + 1) * P], a[:, b, q // 2, (q % 2) * P:(q % 2 + 1) * P], g.ident[:])
                        tr.then_inc(a_turned, 1)
                    if real(n - 2):
                        t.wait_ge(activated, HC * (n - 1))
                        need(t, vec2, CHAIN2 * (n - 3) + 1)
                        for w in range(2):
                            for c in range(HC):
                                mm = t.matmul(ps[:, 7, w * D:(w + 1) * D], ht[:, c, w * P:(w + 1) * P], w2[:, c, :],
                                              start=c == 0, stop=c == HC - 1)
                        mm.then_inc(fed, 1)
                    if real(n - 1):
                        t.wait_ge(x1_ready, n)
                        need(t, x1_copied, n - 1)
                        for c in range(2):
                            for w in range(2):
                                q = 2 * c + w
                                tr = t.transpose(ps[:, 2, q * P:(q + 1) * P], x1[:, 1 - b, w, c * P:(c + 1) * P], g.ident[:])
                        tr.then_inc(x1_turned, 1)
                    if real(n):
                        t.wait_ge(a_copied, n + 1)
                        need(t, vec1, CHAIN1 * (n - 1) + 1)
                        for w in range(2):
                            for c in range(2):
                                mm = t.matmul(ps[:, 1, w * D:(w + 1) * D], at[:, w, c, :], wo[:, c, :], start=c == 0, stop=c == 1)
                        mm.then_inc(attended, 1)
                    if real(n - 1):
                        t.wait_ge(x1_copied, n)
                        for f in range(HC):
                            if f % 2 == 0:
                                need(t, activated, HC * (n - 2) + f + 2)
                            for c in range(2):
                                mm = t.matmul(ps[:, 3 + f // 2, (f % 2) * 2 * P:(f % 2 + 1) * 2 * P],
                                              w1[:, c, f * P:(f + 1) * P], x1t[:, c].rearrange("p w n -> p (w n)"),
                                              start=c == 0, stop=c == 1)
                            mm.then_inc(hidden, 1)

                turns(t, emit)

            @block.scalar
            def _(act):
                act.wait_ge(b1_turned, 1)
                act.copy(b1[:], ps[:, 2, 0:HC]).then_inc(b1_copied, 1)
                act.wait_ge(b1_copied, 1)

                def emit(n, b, i):
                    if real(n):
                        act.wait_ge(a_turned, n + 1)
                        need(act, attended, n)
                        act.copy(at[:].rearrange("p w c n -> p (w c n)"), ps[:, 0, :]).then_inc(a_copied, 1)
                    if real(n - 1):
                        act.wait_ge(x1_turned, n)
                        need(act, hidden, HC * (n - 1))
                        act.copy(x1t[:].rearrange("p c w n -> p (c w n)"), ps[:, 2, :]).then_inc(x1_copied, 1)
                        need(act, fed, n - 1)
                        for f in range(HC):
                            act.wait_ge(hidden, HC * (n - 1) + (f | 1) + 1)
                            act.activation(ht[:, f, :], ps[:, 3 + f // 2, (f % 2) * 2 * P:(f % 2 + 1) * 2 * P], ACT.Gelu,
                                           bias=b1[:, f:f + 1]).then_inc(activated, 1)

                turns(act, emit)

            @block.gpsimd
            def _(pool):
                pool.wait_ge(w_in, 16 * 10)

                def emit(n, b, i):
                    if real(n):
                        pool.wait_ge(x_in[b], 16 * i + 16)
                        need(pool, vec1, CHAIN1 * (n - 2) + 1)
                        nc.gpsimd.tensor_tensor(xb[:, b], x[:, b], both(rows[:, BO]), ALU.add).then_inc(x_biased, 1)
                    if real(n - 2):
                        need(pool, normed, n - 2)
                        pool.wait_ge(vec2, CHAIN2 * (n - 1))
                        nc.gpsimd.tensor_tensor(zg[:], zn[:], both(rows[:, LN2_G]), ALU.mult).then_inc(gained, 1)
                        pool.wait_ge(gained, n - 1)
                        need(pool, stored[b], 16 * (i - 1))
                        nc.gpsimd.tensor_tensor(out[:, b], zg[:], both(rows[:, LN2_B]), ALU.add).then_inc(normed, 1)
                    if real(n):
                        pool.wait_ge(x1_ready, n + 1)
                        nc.gpsimd.tensor_tensor(x1b[:, b], x1[:, b], both(rows[:, B2]), ALU.add).then_inc(x1_biased, 1)

                turns(pool, emit)

            @block.vector
            def _(v):
                v.wait_ge(w_in, 16 * 10)

                def average(n, b):
                    sums = g.sums[:, bass.ds(2 * UROW * n, 2 * UROW)].rearrange("p (w c) -> p w c", w=2)
                    need(v, a_turned, n - 1)
                    v.tensor_scalar(some[:, b], sums[:, :, D:UROW], SOFT_EPS, None, ALU.add).then_inc(shared, 1)
                    v.wait_ge(shared, 2 * n + 1)
                    v.reciprocal(part[:, b], some[:, b]).then_inc(shared, 1)
                    v.wait_ge(shared, 2 * n + 2)
                    v.tensor_tensor(a[:, b].rearrange("p w (h e) -> p w h e", h=HEADS),
                                    sums[:, :, 0:D].rearrange("p w (h e) -> p w h e", h=HEADS),
                                    part[:, b, :, :, None].to_broadcast([P, 2, HEADS, HD]), ALU.mult).then_inc(averaged, 1)

                average(0, 0)

                def emit(n, b, i):
                    if real(n + 1):
                        average(n + 1, 1 - b)
                    if real(n - 2):
                        v.wait_ge(fed, n - 1)
                        v.wait_ge(x1_biased, n - 1)
                        count = CHAIN2 * (n - 2)
                        v.tensor_tensor(y[:], ps[:, 7, :].rearrange("p (w c) -> p w c", w=2), x1b[:, b], ALU.add).then_inc(vec2, 1)
                        v.wait_ge(vec2, count + 1)
                        need(v, gained, n - 2)
                        layer_norm(v, y, scratch, zn, vec2, count + 1)
                    if real(n):
                        v.wait_ge(attended, n + 1)
                        v.wait_ge(x_biased, n + 1)
                        count = CHAIN1 * n
                        v.tensor_tensor(y[:], ps[:, 1, :].rearrange("p (w c) -> p w c", w=2), xb[:, b], ALU.add).then_inc(vec1, 1)
                        v.wait_ge(vec1, count + 1)
                        layer_norm(v, y, scratch, yn, vec1, count + 1)
                        v.tensor_tensor(yg[:], yn[:], both(rows[:, LN1_G]), ALU.mult).then_inc(vec1, 1)
                        v.wait_ge(vec1, count + CHAIN1)
                        v.tensor_tensor(x1[:, b], yg[:], both(rows[:, LN1_B]), ALU.add).then_inc(x1_ready, 1)

                turns(v, emit)

        end_phase(nc, sems)


def last_norms(nc, g):
    with ExitStack() as ctx:
        def sb(name, shape, dt=F32):
            return ctx.enter_context(nc.sbuf_tensor(name, shape, dt))

        def sem(name):
            s = ctx.enter_context(nc.semaphore(name))
            sems.append(s)
            return s

        sems = []
        rows = sb("ln_rows", [P, 2, D])
        x = sb("ln_x", [P, 2, 2, D])
        x1 = sb("ln_x1", [P, 2, 2, D])
        yn = sb("ln_yn", [P, 2, D])
        yg = sb("ln_yg", [P, 2, D])
        yb = sb("ln_yb", [P, 2, D])
        z = sb("ln_z", [P, 2, D])
        scratch = NormTiles(sb, "ln")
        out = sb("ln_out", [P, 2, 2, D])
        w_in, vec = sem("ln_w_in"), sem("ln_vec")
        x_in = [sem(f"ln_x_in{b}") for b in range(2)]
        stored = [sem(f"ln_stored{b}") for b in range(2)]
        STEPS = WINDOWS // 2
        VEC = 2 * NORM_SIGNALS + 3
        left = N - 2 * P * (STEPS - 1)
        assert left <= P
        with nc.Block() as block:

            @block.sync
            def _(sp):
                sp.dma_start(rows[:, 0, :], g.out_g.rearrange("(a d) -> a d", a=1).to_broadcast([P, D])).then_inc(w_in, 16)
                sp.dma_start(rows[:, 1, :], g.out_b.rearrange("(a d) -> a d", a=1).to_broadcast([P, D])).then_inc(w_in, 16)

                def load(n, b):
                    need(sp, vec, VEC * (n - 1))
                    for dram, dest in ((g.x_d, x), (g.x1_d, x1)):
                        sp.dma_start(dest[:, b], dram[bass.ds(2 * P * n, 2 * P), :].rearrange("(a p) c -> p a c", a=2)).then_inc(x_in[b], 16)

                load(0, 0)
                load(1, 1)
                with sp.Fori(1, STEPS // 2) as i:
                    load(2 * i, 0)
                    load(2 * i + 1, 1)
                load(STEPS - 1, 0)

            @block.scalar
            def _(act):
                with act.Fori(0, STEPS // 2) as i:
                    for b in range(2):
                        n = 2 * i + b
                        act.wait_ge(vec, VEC * n + VEC)
                        act.dma_start(g.out[bass.ds(2 * P * n, 2 * P), :].rearrange("(a p) c -> p a c", a=2),
                                      out[:, b]).then_inc(stored[b], 16)
                act.wait_ge(vec, VEC * STEPS)
                act.dma_start(g.out[N - left:N, :], out[0:left, 0, 0, :]).then_inc(stored[0], 16)
                act.wait_ge(stored[0], 16 * ((STEPS + 1) // 2))
                act.wait_ge(stored[1], 16 * (STEPS // 2))

            @block.vector
            def _(v):
                v.wait_ge(w_in, 32)

                def norm(i, b):
                    count = VEC * (2 * i + b)
                    v.wait_ge(x_in[b], 32 * i + 32)
                    layer_norm(v, x[:, b], scratch, yn, vec, count)
                    v.tensor_tensor(yg[:], yn[:], both(rows[:, 0]), ALU.mult).then_inc(vec, 1)
                    v.wait_ge(vec, count + NORM_SIGNALS + 1)
                    v.tensor_tensor(yb[:], yg[:], both(rows[:, 1]), ALU.add).then_inc(vec, 1)
                    v.wait_ge(vec, count + NORM_SIGNALS + 2)
                    v.tensor_tensor(z[:], yb[:], x1[:, b], ALU.add).then_inc(vec, 1)
                    v.wait_ge(vec, count + NORM_SIGNALS + 3)
                    need(v, stored[b], 16 * i)
                    layer_norm(v, z, scratch, out[:, b], vec, count + NORM_SIGNALS + 3)

                norm(0, 0)
                norm(0, 1)
                with v.Fori(1, STEPS // 2) as i:
                    norm(i, 0)
                    norm(i, 1)
                norm(STEPS // 2, 0)

        end_phase(nc, sems)


INPUTS = ["x", "src", "dst", "edge_type_3", "node_type_4", "L0_gnn_W", "L1_gnn_W_Q", "L1_gnn_W_K", "L1_gnn_W_V",
          "L1_gnn_W_E", "L1_gnn_mu", "L1_gnn_Wo", "L1_gnn_bo", "L1_gnn_ln1_g", "L1_gnn_ln1_b", "L1_gnn_ln2_g",
          "L1_gnn_ln2_b", "L1_gnn_w1", "L1_gnn_b1", "L1_gnn_w2", "L1_gnn_b2", "L1_gnn_out_g", "L1_gnn_out_b"]


def gnn_kernel(nc, ins, out):
    g = Shared()
    (g.x, g.src, g.dst, g.edge_type, g.node_type, g.gcn_w, g.w_q, g.w_k, g.w_v, g.w_e, g.mu, g.wo, g.bo, g.ln1_g,
     g.ln1_b, g.ln2_g, g.ln2_b, g.w1, g.b1, g.w2, g.b2, g.out_g, g.out_b) = ins
    g.out = out

    def dram(name, shape, dt=F32):
        return nc.dram_tensor(name, shape, dt, kind="Internal").ap()

    g.x_d = dram("x_state", (NPAD, D))
    g.x1_d = dram("x_first", (NPAD, D))
    g.xs_d = dram("x_scaled", (NPAD, D))
    g.tab_d = dram("kv_table", (EDGE_TYPES, NPAD, ROW))
    g.idx_d = dram("row_indices", (2, BLOCKS, P, TILES), I32)
    g.rec_d = dram("block_records", (BLOCKS, P, REC))
    with ExitStack() as ctx:
        def sb(name, shape, dt=F32):
            return ctx.enter_context(nc.sbuf_tensor(name, shape, dt))

        g.ps = ctx.enter_context(nc.psum_tensor("ps", [P, 8, 512], F32))
        g.ident = sb("ident", [P, P])
        g.iota = sb("iota", [P, P])
        g.ones = sb("ones", [P, P])
        g.zeros = sb("zeros", [P, D])
        g.pair_iota = sb("pair_iota", [P, 4])
        g.same_head = sb("same_head", [P, P])
        g.tile_hot = sb("tile_hot", [P, TILES])
        g.type_hot = sb("type_hot", [P, WINDOWS, NODE_TYPES])
        g.dis = sb("dis", [P, WINDOWS])
        g.keep = sb("keep", [P, PAIRS])
        g.shifts = [0, LAG_COPY, LAG_ADD]
        g.window_rows = sb("window_rows", [P, 3, 480], I32)
        g.sums = sb("sums", [P, (WINDOWS + 1) * UROW])
        g.landed = [ctx.enter_context(nc.semaphore(f"landed{k}")) for k in range(RING)]
        constants(nc, g)
        with nc.sbuf_tensor("before", [P, BLOCKS], F32) as g.before, \
                nc.sbuf_tensor("minus_place", [P, 2 * PAIRS], F32) as g.minus_place, \
                nc.sbuf_tensor("key", [P, 2 * PAIRS], F32) as g.key, \
                nc.sbuf_tensor("idx", [P, 2, BLOCKS, TILES], I32) as g.idx:
            index_pairs(nc, g)
            block_records(nc, g)
        scale_nodes(nc, g)
        gcn_edges(nc, g)
        gcn_nodes(nc, g)
        with nc.Fori(0, LAYERS) as layer:
            project(nc, g, layer)
            attention_edges(nc, g, layer)
            attention_nodes(nc, g, layer)
        last_norms(nc, g)


def kernel(**inputs):
    import numpy as _np
    import concourse.bacc as _bacc
    from concourse import mybir as _mybir
    from concourse.bass_utils import run_bass_kernel_spmd as _run

    nc = _bacc.Bacc("TRN2", target_bir_lowering=False, num_devices=1)
    arrays, args = {}, []
    for name in INPUTS:
        a = _np.ascontiguousarray(inputs[name])
        arrays[f"in_{name}"] = a
        args.append(nc.dram_tensor(f"in_{name}", a.shape, _mybir.dt.from_np(a.dtype), kind="ExternalInput").ap())
    out = nc.dram_tensor("out_0", (N, D), _mybir.dt.float32, kind="ExternalOutput").ap()
    gnn_kernel(nc, args, out)
    r = _run(nc, [arrays], core_ids=[0])
    return r.results[0]["out_0"]
```

```python
import concourse.bass as bass
from concourse import mybir
from contextlib import ExitStack

F32 = mybir.dt.float32
I32 = mybir.dt.int32
BF16 = mybir.dt.bfloat16
ALU = mybir.AluOpType
ACT = mybir.ActivationFunctionType
AX = mybir.AxisListType
PE_ENGINE = mybir.EngineType.PE
DVE_ENGINE = mybir.EngineType.DVE

P = 128
N, E, D = 6250, 100000, 256
LAYERS, HEADS, HD = 3, 8, 32
NODE_TYPES, EDGE_TYPES = 4, 3
HIDDEN = 4 * D
WINDOWS = 50
NPAD = WINDOWS * P
GROUP = 2 * P
GROUPS = -(-E // GROUP)
CHUNKS = -(-(GROUPS + 1) // P)
NO_GROUP = 440
BLOCK = 8
TILES = 2 * BLOCK
PAIRS = 448
BLOCKS = PAIRS // BLOCK
ROUNDS = BLOCKS // 2
RING = 16
PASS_LANDED = 32 * ROUNDS
assert GROUPS + WINDOWS - 1 <= PAIRS and GROUPS <= NO_GROUP < CHUNKS * P
NOWHERE = 8191
BIG = 3.0e38
FLOOR = -1.0e9
EPS = 1e-5
SOFT_EPS = 1e-10

ROW = 2 * D
SLOT = ROW + HEADS
UROW = D + HEADS
PROJ = 2 + EDGE_TYPES

REC_PEN, REC_FIRST, REC_LAST, REC_CROSS = 0, 129, 257, 385
CROSS = 2 * TILES + 1
REC_CARRY = REC_CROSS + 2 * CROSS
REC_PLACE = REC_CARRY + 1
REC = REC_PLACE + TILES


def need(eng, sem, value):
    if isinstance(value, int) and value <= 0:
        return
    eng.wait_ge(sem, value)


def need_apart(eng, sem, value):
    if isinstance(value, int) and value <= 0:
        return
    eng.wait_ge(sem, value)
    eng.nop(nofuse=True)


def end_phase(nc, sems):
    for s in sems:
        nc.sync.sem_clear(s)
    nc.all_engine_barrier()


def load_words(nc, row, engine, start, count):
    _, words = nc.values_load_multi_w_load_instructions(
        row[0:1, bass.ds(start, count)], [engine],
        skip_runtime_bounds_check_because="windows are clamped to 0..WINDOWS-1 where they are computed")
    return words


RSQRT_SIGNALS = 11
SEED = 0x5F3759DF


def reciprocal_sqrt(v, value, root, bits, half, done, count):
    at = [count]

    def then(inst):
        at[0] += 1
        inst.then_inc(done, 1)
        v.wait_ge(done, at[0])

    then(v.tensor_single_scalar(bits, value.bitcast(I32), 1, ALU.arith_shift_right))
    then(v.tensor_scalar(root.bitcast(I32), bits, -1.0, float(SEED), ALU.mult, ALU.add))
    for _ in range(3):
        then(v.tensor_tensor(half, value, root, ALU.mult))
        then(v.scalar_tensor_tensor(out=half, in0=half, scalar=-0.5, in1=root, op0=ALU.mult, op1=ALU.mult))
        then(v.scalar_tensor_tensor(out=root, in0=half, scalar=1.5, in1=root, op0=ALU.add, op1=ALU.mult))


class Shared:
    pass


def constants(nc, g):
    with ExitStack() as ctx:
        diff = ctx.enter_context(nc.sbuf_tensor("diff", [P, P], I32))
        type_rows = ctx.enter_context(nc.sbuf_tensor("type_rows", [WINDOWS, P], I32))
        type_rows_f = ctx.enter_context(nc.sbuf_tensor("type_rows_f", [WINDOWS, P], F32))
        type_col = ctx.enter_context(nc.sbuf_tensor("type_col", [P, WINDOWS], F32))
        made = ctx.enter_context(nc.semaphore("const_made"))
        masks = ctx.enter_context(nc.semaphore("const_masks"))
        cleared = ctx.enter_context(nc.semaphore("const_cleared"))
        loaded = ctx.enter_context(nc.semaphore("const_loaded"))
        turned = ctx.enter_context(nc.semaphore("const_turned"))
        whole = N // P
        with nc.Block() as block:

            @block.sync
            def _(sp):
                sp.wait_ge(cleared, 1)
                sp.dma_start(type_rows[0:whole, :],
                             g.node_type[0:whole * P].rearrange("(w p) -> w p", p=P)).then_inc(loaded, 16)
                sp.dma_start(type_rows[whole:whole + 1, 0:N - whole * P],
                             g.node_type[whole * P:N].rearrange("(w p) -> w p", w=1)).then_inc(loaded, 16)

            @block.tensor
            def _(t):
                t.wait_ge(made, 6)
                t.wait_ge(masks, 3)
                t.transpose(g.ps[:, 0, 0:WINDOWS], type_rows_f[:], g.ident[0:WINDOWS, 0:WINDOWS]).then_inc(turned, 1)

            @block.gpsimd
            def _(pool):
                nc.gpsimd.memset(g.ident[:], 0.0).then_inc(made, 1)
                nc.gpsimd.memset(g.tile_hot[:], 1.0).then_inc(made, 1)
                pool.wait_ge(made, 2)
                nc.gpsimd.affine_select(out=g.ident[:], in_=g.ident[:], compare_op=ALU.not_equal, fill=1.0,
                                        base=0, pattern=[[-1, P]], channel_multiplier=1).then_inc(made, 1)
                nc.gpsimd.affine_select(out=g.tile_hot[:], in_=g.tile_hot[:], compare_op=ALU.is_ge, fill=0.0,
                                        base=0, pattern=[[-HEADS, TILES]], channel_multiplier=1).then_inc(made, 1)
                pool.wait_ge(made, 4)
                nc.gpsimd.affine_select(out=g.tile_hot[:], in_=g.tile_hot[:], compare_op=ALU.is_ge, fill=0.0,
                                        base=HEADS - 1, pattern=[[HEADS, TILES]],
                                        channel_multiplier=-1).then_inc(made, 1)
                nc.gpsimd.iota(g.iota[:], [[1, P]], 0, 0, allow_small_or_imprecise_dtypes=True)
                nc.gpsimd.iota(g.pair_iota[:], [[P, 4]], 0, 1, allow_small_or_imprecise_dtypes=True)
                nc.gpsimd.iota(diff[:], [[-1, P]], P, 1).then_inc(made, 1)

            @block.vector
            def _(v):
                v.memset(type_rows[:], 0).then_inc(cleared, 1)
                v.memset(g.ones[:], 1.0)
                v.memset(g.zeros[:], 0.0)
                v.memset(g.sums[:, (N // P) * D:], 0.0)
                v.wait_ge(made, 6)
                v.tensor_single_scalar(diff[:], diff[:], HEADS - 1, ALU.bitwise_and).then_inc(masks, 1)
                v.wait_ge(masks, 1)
                v.tensor_single_scalar(g.same_head[:], diff[:], 0, ALU.is_equal).then_inc(masks, 1)
                v.tensor_scalar(g.minus_ident[:], g.ident[:], -1.0, None, ALU.mult)
                v.wait_ge(loaded, 32)
                v.tensor_copy(type_rows_f[:], type_rows[:]).then_inc(masks, 1)
                v.wait_ge(turned, 1)
                v.tensor_copy(type_col[:], g.ps[:, 0, 0:WINDOWS]).then_inc(masks, 1)
                v.wait_ge(masks, 4)
                for k in range(NODE_TYPES):
                    v.tensor_scalar(g.type_hot[:, :, k], type_col[:], float(k), None, ALU.is_equal)

        end_phase(nc, [made, masks, cleared, loaded, turned])


def index_pairs(nc, g):
    with ExitStack() as ctx:
        def sb(name, shape, dt=F32):
            return ctx.enter_context(nc.sbuf_tensor(name, shape, dt))

        def sem(name):
            s = ctx.enter_context(nc.semaphore(name))
            sems.append(s)
            return s

        sems = []
        raw = sb("raw", [P, 3, CHUNKS, GROUP], I32)
        part = sb("part", [P, 2, CHUNKS, GROUP], I32)
        val = sb("val", [P, 3, CHUNKS, GROUP])
        typ = sb("typ", [P, CHUNKS, GROUP])
        partf = sb("partf", [P, 2, CHUNKS, GROUP])
        cols = sb("cols", [P, 2, 2 * CHUNKS, P])
        place_hot = sb("place_hot", [P, 2, 16, P], BF16)
        window_hot = sb("window_hot", [P, 2, 16, WINDOWS], BF16)
        deg = sb("deg", [P, WINDOWS])
        cnt = sb("cnt", [P, WINDOWS])
        work = sb("work", [P, 12, WINDOWS])
        ints = sb("ints", [P, 2, WINDOWS], I32)
        mask = sb("mask", [P, 4, 4, WINDOWS])
        pv = sb("pv", [P, 12, 4])
        diag = sb("diag", [P, 12, P])
        prow = sb("prow", [P, 3, 512])
        pick = sb("pick", [P, CHUNKS, 512])
        got = sb("got", [P, 3, 512, 2])
        place = sb("place", [P, 512, 2])
        flag = sb("flag", [P, 3, 512, 2])
        dist = sb("ix_dist", [P, 2, 16, WINDOWS])
        x_in, scales_ready, scaled, dist_ready, far_ready, window_ready, placed = (
            sem("ix_x_in"), sem("ix_scales"), sem("ix_scaled"), sem("ix_dist"), sem("ix_far"),
            sem("ix_window_hot"), sem("ix_placed"))
        CHUNK = 5
        x_rows = g.sums[:, 0:WINDOWS * D].rearrange("p (w c) -> p w c", c=D)
        loaded, pad_set, vec, turned, columned, hot_ready, hot_used = (
            sem("ix_loaded"), sem("ix_pad"), sem("ix_vec"), sem("ix_turned"), sem("ix_columned"),
            sem("ix_hot"), sem("ix_hot_used"))
        parted, counted, deg_ready, diag_ready, spread, pick_ready, picked, evac, stored, idx_ready = (
            sem("ix_parted"), sem("ix_counted"), sem("ix_deg"), sem("ix_diag"), sem("ix_spread"),
            sem("ix_pick"), sem("ix_picked"), sem("ix_evac"), sem("ix_stored"), sem("ix_idx"))
        ps = g.ps
        full = (E // GROUP) // P
        tail = E // GROUP - full * P
        rest = E - (E // GROUP) * GROUP
        HIST = full * 2 * P // 16
        with nc.Block() as block:

            @block.sync
            def _(sp):
                for a, src in enumerate((g.dst, g.src, g.edge_type)):
                    sp.dma_start(raw[:, a, 0:full, :],
                                 src[0:full * P * GROUP].rearrange("(c s e) -> s c e", c=full, s=P)).then_inc(loaded, 16)
                sp.wait_ge(pad_set, 2)
                for a, src in enumerate((g.dst, g.src, g.edge_type)):
                    sp.dma_start(raw[0:tail, a, full, :],
                                 src[full * P * GROUP:E - rest].rearrange("(s e) -> s e", e=GROUP)).then_inc(loaded, 16)
                    sp.dma_start(raw[tail:tail + 1, a, full, 0:rest],
                                 src[E - rest:E].rearrange("(s e) -> s e", s=1)).then_inc(loaded, 16)
                sp.dma_start(g.x_d[0:N, :], g.x).then_inc(stored, 16)
                sp.dma_start(g.x_d[N:N + P, :], g.zeros[:, 0:D]).then_inc(stored, 16)
                sp.dma_start(g.x_d[N + P:NPAD, :], g.zeros[0:NPAD - N - P, 0:D]).then_inc(stored, 16)
                whole = N // P
                for w0 in range(0, whole, 2 * CHUNK):
                    w1 = min(w0 + 2 * CHUNK, whole)
                    sp.dma_start(x_rows[:, w0:w1, :], g.x[w0 * P:w1 * P, :].rearrange("(w p) c -> p w c", p=P)).then_inc(x_in, 16)
                sp.dma_start(x_rows[0:N - whole * P, whole, :], g.x[whole * P:N, :]).then_inc(x_in, 16)
                for k in range(WINDOWS // CHUNK):
                    sp.wait_ge(scaled, k + 1)
                    sp.dma_start(g.xs_d[k * CHUNK * P:(k + 1) * CHUNK * P, :].rearrange("(w p) c -> p w c", p=P),
                                 x_rows[:, k * CHUNK:(k + 1) * CHUNK, :]).then_inc(stored, 16)
                sp.wait_ge(idx_ready, 1)
                for kind in range(2):
                    for half in range(2):
                        b0, b1 = half * BLOCKS // 2, (half + 1) * BLOCKS // 2
                        sp.dma_start(g.idx_d[kind, b0:b1].rearrange("b p t -> p b t"),
                                     g.idx[:, kind, b0:b1, :]).then_inc(stored, 16)
                sp.wait_ge(placed, 1)
                sp.dma_start(g.place_d.rearrange("b p t -> p b t"),
                             g.minus_place[:].rearrange("p (b t) -> p b t", t=TILES)).then_inc(stored, 16)
                sp.wait_ge(stored, 16 * (8 + WINDOWS // CHUNK))

            @block.tensor
            def _(t):
                t.wait_ge(parted, 1)
                for a in range(2):
                    for half in range(2):
                        k = 2 * a + half
                        for q in range(4):
                            c, j = divmod(4 * half + q, 2)
                            tr = t.transpose(ps[:, k, q * P:(q + 1) * P], partf[:, a, c, j * P:(j + 1) * P], g.ident[:])
                        tr.then_inc(turned, 1)
                def histogram(turn, buf, first, last):
                    t.wait_ge(hot_ready, turn + 1)
                    t.wait_ge(window_ready, turn + 1)
                    for u in range(16):
                        mm = t.matmul(ps[:, 4, 0:WINDOWS], place_hot[:, buf, u, :], window_hot[:, buf, u, :],
                                      start=first and u == 0, stop=last and u == 15, skip_group_check=True)
                    mm.then_inc(hot_used, 1)

                histogram(0, 0, True, False)
                histogram(1, 1, False, False)
                with t.Fori(1, HIST // 2) as i:
                    histogram(2 * i, 0, False, False)
                    histogram(2 * i + 1, 1, False, False)
                histogram(HIST, 0, False, False)
                histogram(HIST + 1, 1, False, True)
                t.wait_ge(deg_ready, 1)
                t.matmul(ps[:, 5, 0:WINDOWS], g.ones[:, 0:P], cnt[:], start=True, stop=True).then_inc(counted, 1)
                t.wait_ge(diag_ready, 1)
                for a in range(3):
                    for q in range(4):
                        mm = t.matmul(ps[:, a, q * P:(q + 1) * P], g.ones[:, 0:P], diag[:, 4 * a + q, :],
                                      start=True, stop=True)
                    mm.then_inc(spread, 1)
                t.wait_ge(pick_ready, 1)
                for a in range(3):
                    for j in range(2):
                        k = 2 * a + j
                        for c in range(CHUNKS):
                            mm = t.matmul(ps[:, 2 + k, :], val[:, a, c, j * P:(j + 1) * P], pick[:, c, :],
                                          start=c == 0, stop=c == CHUNKS - 1)
                        mm.then_inc(picked, 1)

            @block.gpsimd
            def _(pool):
                pool.wait_ge(columned, 4)

                def distance(turn, buf, tiles):
                    need_apart(pool, window_ready, turn - 1)
                    nc.gpsimd.tensor_tensor(dist[:, buf], tiles[:, :, None].to_broadcast([P, 16, WINDOWS]),
                                            g.iota[:, None, 0:WINDOWS].to_broadcast([P, 16, WINDOWS]),
                                            ALU.subtract).then_inc(dist_ready, 1)

                flat = cols[:, 0].rearrange("p c s -> p (c s)")
                distance(0, 0, flat[:, 0:16])
                distance(1, 1, flat[:, 16:32])
                with pool.Fori(1, HIST // 2) as i:
                    for b in range(2):
                        distance(2 * i + b, b, flat[:, bass.ds(32 * i + 16 * b, 16)])
                distance(HIST, 0, cols[:, 0, 2 * full, 0:16])
                distance(HIST + 1, 1, cols[:, 0, 2 * full + 1, 0:16])
                pool.wait_ge(x_in, 16 * (-(-(N // P) // (2 * CHUNK)) + 1))
                pool.wait_ge(scales_ready, 1)
                for k in range(WINDOWS // CHUNK):
                    rows = x_rows[:, k * CHUNK:(k + 1) * CHUNK, :]
                    nc.gpsimd.tensor_tensor(rows, rows, g.dis[:, k * CHUNK:(k + 1) * CHUNK, None]
                                            .to_broadcast([P, CHUNK, D]), ALU.mult).then_inc(scaled, 1)

            @block.scalar
            def _(act):
                for k in range(4):
                    a, half = divmod(k, 2)
                    act.wait_ge(turned, k + 1)
                    act.copy(cols[:, a, 4 * half:4 * half + 4, :],
                             ps[:, k, :].rearrange("p (q s) -> p q s", q=4)).then_inc(columned, 1)

                def hots(turn, buf):
                    act.wait_ge(dist_ready, turn + 1)
                    act.activation(dist[:, buf], dist[:, buf], ACT.Abs).then_inc(far_ready, 1)
                    need(act, hot_used, turn - 1)
                    act.wait_ge(far_ready, turn + 1)
                    act.activation(window_hot[:, buf], dist[:, buf], ACT.Relu, bias=1.0, scale=-1.0).then_inc(window_ready, 1)

                hots(0, 0)
                hots(1, 1)
                with act.Fori(1, HIST // 2) as i:
                    hots(2 * i, 0)
                    hots(2 * i + 1, 1)
                hots(HIST, 0)
                hots(HIST + 1, 1)
                for k in range(6):
                    a, j = divmod(k, 2)
                    act.wait_ge(picked, k + 1)
                    act.copy(got[:, a, :, j], ps[:, 2 + k, :]).then_inc(evac, 1)

            @block.vector
            def _(v):
                steps = [0]

                def then(inst):
                    steps[0] += 1
                    inst.then_inc(vec, 1)
                    v.wait_ge(vec, steps[0])

                v.memset(raw[:, 0, full, :], NOWHERE).then_inc(pad_set, 1)
                v.memset(raw[:, 1:3, full, :], 0).then_inc(pad_set, 1)
                v.wait_ge(loaded, 16 * 9)
                v.tensor_single_scalar(part[:, 0], raw[:, 0], 7, ALU.arith_shift_right)
                then(v.tensor_single_scalar(part[:, 1], raw[:, 0], P - 1, ALU.bitwise_and))
                v.tensor_copy(partf[:], part[:]).then_inc(parted, 1)
                v.tensor_copy(val[:, 0:2], raw[:, 0:2])
                then(v.tensor_copy(typ[:], raw[:, 2]))
                v.scalar_tensor_tensor(out=val[:, 2], in0=typ[:], scalar=float(NPAD), in1=val[:, 1],
                                       op0=ALU.mult, op1=ALU.add)
                v.wait_ge(columned, 4)

                def hots(turn, buf, tiles):
                    need(v, hot_used, turn - 1)
                    v.tensor_tensor(place_hot[:, buf], tiles[:, :, None].to_broadcast([P, 16, P]),
                                    g.iota[:, None, :].to_broadcast([P, 16, P]), ALU.is_equal).then_inc(hot_ready, 1)

                flat = cols[:, 1].rearrange("p c s -> p (c s)")
                hots(0, 0, flat[:, 0:16])
                hots(1, 1, flat[:, 16:32])
                with v.Fori(1, HIST // 2) as i:
                    for b in range(2):
                        hots(2 * i + b, b, flat[:, bass.ds(32 * i + 16 * b, 16)])
                hots(HIST, 0, cols[:, 1, 2 * full, 0:16])
                hots(HIST + 1, 1, cols[:, 1, 2 * full + 1, 0:16])
                v.wait_ge(hot_used, HIST + 2)
                then(v.tensor_copy(deg[:], ps[:, 4, 0:WINDOWS]))
                then(v.tensor_scalar(work[:, 0], deg[:], 1.0, None, ALU.max))
                v.tensor_copy(cnt[:], deg[:]).then_inc(deg_ready, 1)
                reciprocal_sqrt(v, work[:, 0], work[:, 1], ints[:, 0], work[:, 11], vec, steps[0])
                steps[0] += RSQRT_SIGNALS
                v.scalar_tensor_tensor(out=g.dis[:], in0=deg[:], scalar=0.0, in1=work[:, 1],
                                       op0=ALU.is_gt, op1=ALU.mult).then_inc(scales_ready, 1)
                v.wait_ge(counted, 1)
                COUNT, END, START, G0, G1, NP, PEND, PST, OFF = 2, 3, 4, 5, 6, 7, 8, 9, 10
                then(v.tensor_copy(work[:, COUNT], ps[:, 5, 0:WINDOWS]))
                then(v.tensor_tensor_scan(work[:, END], work[:, COUNT], g.zeros[:, 0:WINDOWS], 0.0, ALU.add, ALU.add))
                then(v.tensor_tensor(work[:, START], work[:, END], work[:, COUNT], ALU.subtract))
                v.tensor_copy(ints[:, 0], work[:, START])
                then(v.tensor_scalar(ints[:, 1], work[:, END], -1.0, None, ALU.add))
                v_ints = ints[:].rearrange("p a w -> p (a w)")
                then(v.tensor_single_scalar(v_ints, v_ints, 8, ALU.arith_shift_right))
                then(v.tensor_copy(work[:, G0:G1 + 1], ints[:]))
                then(v.tensor_tensor(work[:, NP], work[:, G1], work[:, G0], ALU.subtract))
                then(v.scalar_tensor_tensor(out=work[:, NP], in0=work[:, COUNT], scalar=0.0, in1=work[:, NP],
                                            op0=ALU.is_gt, op1=ALU.mult))
                then(v.tensor_scalar(work[:, NP], work[:, NP], 1.0, None, ALU.add))
                then(v.tensor_tensor_scan(work[:, PEND], work[:, NP], g.zeros[:, 0:WINDOWS], 0.0, ALU.add, ALU.add))
                then(v.tensor_tensor(work[:, PST], work[:, PEND], work[:, NP], ALU.subtract))
                then(v.tensor_scalar(work[:, G0], work[:, G0], float(GROUPS - 1), None, ALU.min))
                then(v.tensor_tensor(work[:, OFF], work[:, G0], work[:, PST], ALU.subtract))
                shape = [P, 4, WINDOWS]

                def windows_row(k):
                    return work[:, k, None, :].to_broadcast(shape)

                pairs_col = g.pair_iota[:, :, None].to_broadcast(shape)
                then(v.tensor_tensor(mask[:, 0], windows_row(PEND), pairs_col, ALU.is_le))
                then(v.tensor_reduce(pv[:, 0], mask[:, 0], AX.X, ALU.add))
                then(v.tensor_tensor(mask[:, 1], g.iota[:, None, 0:WINDOWS].to_broadcast(shape),
                                     pv[:, 0, :, None].to_broadcast(shape), ALU.is_equal))
                v.tensor_tensor(mask[:, 2], mask[:, 1], windows_row(OFF), ALU.mult)
                then(v.tensor_tensor(mask[:, 3], mask[:, 1], windows_row(PST), ALU.mult))
                v.tensor_reduce(pv[:, 1], mask[:, 2], AX.X, ALU.add)
                then(v.tensor_reduce(pv[:, 2], mask[:, 3], AX.X, ALU.add))
                GRP, WIN, KEEP = 8, 9, 10
                then(v.tensor_tensor(pv[:, 3], pv[:, 1], g.pair_iota[:], ALU.add))
                then(v.tensor_scalar(pv[:, 4], pv[:, 0], float(WINDOWS), None, ALU.is_lt))
                then(v.tensor_scalar(pv[:, 3], pv[:, 3], -float(NO_GROUP), None, ALU.add))
                then(v.tensor_tensor(pv[:, 3], pv[:, 3], pv[:, 4], ALU.mult))
                v.tensor_scalar(pv[:, GRP], pv[:, 3], float(NO_GROUP), None, ALU.add)
                v.tensor_scalar(pv[:, WIN], pv[:, 0], float(WINDOWS - 1), None, ALU.min)
                then(v.tensor_tensor(pv[:, KEEP], pv[:, 2], g.pair_iota[:], ALU.not_equal))
                for k in range(12):
                    a, q = divmod(k, 4)
                    d = v.tensor_scalar(diag[:, k], g.ident[:], pv[:, GRP + a, q:q + 1], None, ALU.mult)
                d.then_inc(diag_ready, 1)
                v.wait_ge(spread, 3)
                then(v.tensor_copy(prow[:], ps[:, 0:3, :]))
                for c in range(CHUNKS):
                    d = v.tensor_scalar(pick[:, c], prow[:, 0], g.pair_iota[:, c:c + 1], None, ALU.is_equal)
                d.then_inc(pick_ready, 1)
                v.tensor_copy(g.keep[:], prow[:, 2, 0:PAIRS])
                v.memset(g.window_rows[:], 0).then_inc(pad_set, 1)
                v.wait_ge(pad_set, 3)
                for k, shift in enumerate(g.shifts):
                    v.tensor_copy(g.window_rows[0:1, k, shift:shift + PAIRS], prow[0:1, 1, 0:PAIRS])
                v.memset(g.before[:, 0:1], 1.0)
                v.tensor_scalar(g.before[:, 1:BLOCKS], prow[:, 1, BLOCK - 1:PAIRS - 1:BLOCK], -float(P), 1.0,
                                ALU.mult, ALU.add)
                v.wait_ge(evac, 6)
                then(v.scalar_tensor_tensor(out=place[:], in0=prow[:, 1, :, None].to_broadcast([P, 512, 2]),
                                            scalar=-float(P), in1=got[:, 0], op0=ALU.mult, op1=ALU.add))
                in_block = g.idx[:].rearrange("p k b t -> p k (b t)")
                v.tensor_copy(in_block[:, 0], got[:, 1].rearrange("p q j -> p (q j)")[:, 0:2 * PAIRS])
                v.tensor_copy(in_block[:, 1], got[:, 2].rearrange("p q j -> p (q j)")[:, 0:2 * PAIRS]).then_inc(idx_ready, 1)
                pl = place[:].rearrange("p q j -> p (q j)")[:, 0:2 * PAIRS]
                v.tensor_scalar(g.minus_place[:], pl, -1.0, None, ALU.mult).then_inc(placed, 1)
                fl = [flag[:, k].rearrange("p q j -> p (q j)")[:, 0:2 * PAIRS] for k in range(3)]
                then(v.tensor_scalar(fl[0], pl, 0.0, None, ALU.is_ge))
                then(v.scalar_tensor_tensor(out=fl[1], in0=pl, scalar=float(P), in1=fl[0], op0=ALU.is_lt, op1=ALU.mult))
                then(v.scalar_tensor_tensor(out=fl[2], in0=got[:, 0].rearrange("p q j -> p (q j)")[:, 0:2 * PAIRS],
                                            scalar=1.0, in1=fl[1], op0=ALU.add, op1=ALU.mult))
                then(v.tensor_scalar(g.key[:], fl[2], -1.0, None, ALU.add))

        end_phase(nc, sems)


def gcn_edges(nc, g):
    with ExitStack() as ctx:
        def sb(name, shape, dt=F32):
            return ctx.enter_context(nc.sbuf_tensor(name, shape, dt))

        def sem(name):
            s = ctx.enter_context(nc.semaphore(name))
            sems.append(s)
            return s

        sems = []
        rows = sb("gc_rows", [P, 2 * RING, D])
        hot = sb("gc_hot", [P, RING, 2, P])
        dist = sb("gc_dist", [P, 2, 2, P])
        idx = sb("gc_idx", [P, 2, TILES], I32)
        place = sb("gc_place", [P, 2, TILES])
        idx_in = [sem(f"gc_idx_in{b}") for b in range(2)]
        place_in = [sem(f"gc_place_in{b}") for b in range(2)]
        landed = g.landed
        dist_ready, hot_ready, summed, added = sem("gc_dist_ready"), sem("gc_hot_ready"), sem("gc_summed"), sem("gc_added")
        DUO = RING // BLOCK
        by_head = sb("br_by_head", [P, DUO * TILES, HEADS])
        kt = sb("br_kt", [P, DUO, P])
        ends = sb("br_ends", [P, DUO, CROSS])
        last_key = sb("br_last_key", [P, 1])
        carry = sb("br_carry", [P, 2, DUO])
        rec = sb("br_rec", [P, DUO, REC])
        keyed, turned, copied, ends_ready, crossed, vec, rec_ready, stored = (
            sem("br_keyed"), sem("br_turned"), sem("br_copied"), sem("br_ends"), sem("br_crossed"),
            sem("br_vec"), sem("br_rec"), sem("br_stored"))
        KEY_BANK, CROSS_BANK = 2, 3
        AT_KEYS, AT_TURN, AT_COPY, AT_ENDS, AT_CROSS, AT_RECORD = 1, 3, 5, 7, 9, 11

        with nc.Block() as block:

            @block.sync
            def _(sp):
                def load_block(i, b):
                    blk = 2 * i + b
                    need(sp, summed, BLOCK * (blk - 1))
                    need(sp, hot_ready, BLOCK * (blk - 1))
                    sp.dma_start(idx[:, b, :], g.idx_d[0, bass.ds(blk, 1)].rearrange("b p t -> (b p) t")).then_inc(idx_in[b], 16)
                    sp.dma_start(place[:, b, :], g.place_d[bass.ds(blk, 1)].rearrange("b p t -> (b p) t")).then_inc(place_in[b], 16)

                def store_records(i):
                    sp.wait_ge(rec_ready, i + 1)
                    sp.dma_start(g.rec_d[bass.ds(DUO * i, DUO)].rearrange("b p r -> p b r"), rec[:]).then_inc(stored, 16)

                load_block(0, 0)
                load_block(0, 1)
                with sp.Fori(1, ROUNDS) as i:
                    load_block(i, 0)
                    load_block(i, 1)
                    store_records(i - 1)
                store_records(ROUNDS - 1)
                sp.wait_ge(stored, 16 * ROUNDS)

            @block.gpsimd
            def _(pool):
                def gather(i):
                    for k in range(RING):
                        b, u = divmod(k, BLOCK)
                        if u == 0:
                            need_apart(pool, idx_in[b], 16 * i + 16)
                        need_apart(pool, summed, RING * i + k - RING + 1)
                        for j in range(2):
                            nc.gpsimd.indirect_dma_start(
                                rows[:, 2 * k + j, :], None, g.xs_d,
                                bass.IndirectOffsetOnAxis(idx[:, b, 2 * u + j:2 * u + j + 1], 0)).then_inc(landed[k], 16)

                gather(0)
                with pool.Fori(1, ROUNDS) as i:
                    gather(i)

            @block.scalar
            def _(act):
                def one_hots(i):
                    for k in range(RING):
                        b, u = divmod(k, BLOCK)
                        n = RING * i + k
                        if u == 0:
                            need(act, place_in[b], 16 * i + 16)
                        for j in range(2):
                            d = act.activation(dist[:, k % 2, j, :], g.iota[:], ACT.Abs,
                                               bias=place[:, b, 2 * u + j:2 * u + j + 1])
                        d.then_inc(dist_ready, 1)
                        need(act, summed, n - RING + 1)
                        act.wait_ge(dist_ready, n + 1)
                        act.activation(hot[:, k], dist[:, k % 2], ACT.Relu, bias=1.0, scale=-1.0).then_inc(hot_ready, 1)
                        if k == AT_COPY:
                            act.wait_ge(turned, i + 1)
                            act.copy(kt[:].rearrange("p q e -> p (q e)"), g.ps[:, KEY_BANK, 0:DUO * P]).then_inc(copied, 1)

                one_hots(0)
                with act.Fori(1, ROUNDS) as i:
                    one_hots(i)

            @block.tensor
            def _(t):
                def sums(i):
                    for k in range(RING):
                        n = RING * i + k
                        t.wait_ge(hot_ready, n + 1)
                        t.wait_ge(landed[k], 32 * i + 32)
                        need(t, added, n - 1)
                        for j in range(2):
                            mm = t.matmul(g.ps[:, k % 2, 0:D], hot[:, k, j, :], rows[:, 2 * k + j, :],
                                          start=j == 0, stop=j == 1)
                        mm.then_inc(summed, 1)
                        if k == AT_TURN:
                            t.wait_ge(keyed, i + 1)
                            for q in range(DUO):
                                tr = t.transpose(g.ps[:, KEY_BANK, q * P:(q + 1) * P],
                                                 by_head[:, q * TILES:(q + 1) * TILES, :].rearrange("p t h -> p (t h)"), g.ident[:])
                            tr.then_inc(turned, 1)
                        if k == AT_CROSS:
                            t.wait_ge(ends_ready, i + 1)
                            t.matmul(g.ps[:, CROSS_BANK, 0:DUO * CROSS], g.same_head[:], ends[:].rearrange("p q c -> p (q c)"),
                                     start=True, stop=True).then_inc(crossed, 1)

                sums(0)
                with t.Fori(1, ROUNDS) as i:
                    sums(i)

            @block.vector
            def _(v):
                v.memset(last_key[:], -2.0)
                v.memset(rec[:], -BIG).then_inc(vec, 1)
                v.wait_ge(vec, 1)
                SIGNALS = 5

                def edge_keys(i):
                    tiles = g.key[:, bass.ds(DUO * TILES * i, DUO * TILES)]
                    v.tensor_copy(by_head[:], tiles[:, :, None].to_broadcast([P, DUO * TILES, HEADS])).then_inc(keyed, 1)

                def tile_ends(i):
                    v.wait_ge(copied, i + 1)
                    own = g.tile_hot[:, None, :].to_broadcast([P, DUO, TILES])
                    v.tensor_tensor(ends[:, :, 0:TILES], own, kt[:, :, 0:1].to_broadcast([P, DUO, TILES]), ALU.mult)
                    v.tensor_tensor(ends[:, :, TILES:2 * TILES], own, kt[:, :, P - 1:P].to_broadcast([P, DUO, TILES]),
                                    ALU.mult)
                    v.tensor_tensor(ends[:, 0, CROSS - 1:CROSS], g.tile_hot[:, TILES - 1:TILES], last_key[:], ALU.mult)
                    v.tensor_tensor(ends[:, 1:DUO, CROSS - 1:CROSS],
                                    g.tile_hot[:, None, TILES - 1:TILES].to_broadcast([P, DUO - 1, 1]),
                                    kt[:, 0:DUO - 1, P - 1:P], ALU.mult).then_inc(vec, 1)
                    v.wait_ge(vec, SIGNALS * i + 2)
                    v.tensor_copy(last_key[:], kt[:, DUO - 1, P - 1:P]).then_inc(ends_ready, 1)

                def record(i):
                    signals = [SIGNALS * i + 2]

                    def then(inst):
                        signals[0] = signals[0] + 1
                        inst.then_inc(vec, 1)
                        v.wait_ge(vec, signals[0])

                    places = g.minus_place[:, bass.ds(DUO * TILES * i, DUO * TILES)]
                    before = g.before[:, bass.ds(DUO * i, DUO)]
                    need(v, stored, 16 * i)
                    v.tensor_tensor(rec[:, :, REC_PEN + 1:REC_PEN + P], kt[:, :, 1:P], kt[:, :, 0:P - 1], ALU.not_equal)
                    v.tensor_tensor(rec[:, :, REC_FIRST:REC_FIRST + P], kt[:], kt[:, :, 0:1].to_broadcast([P, DUO, P]),
                                    ALU.not_equal)
                    v.tensor_tensor(rec[:, :, REC_LAST:REC_LAST + P], kt[:], kt[:, :, P - 1:P].to_broadcast([P, DUO, P]),
                                    ALU.not_equal)
                    v.wait_ge(crossed, i + 1)
                    cross = g.ps[:, CROSS_BANK, 0:DUO * CROSS].rearrange("p (q c) -> p q c", q=DUO)
                    v.tensor_tensor(rec[:, :, REC_CROSS:REC_CROSS + CROSS], cross,
                                    kt[:, :, 0:1].to_broadcast([P, DUO, CROSS]), ALU.not_equal)
                    v.tensor_tensor(rec[:, :, REC_CROSS + CROSS:REC_CARRY], cross,
                                    kt[:, :, P - 1:P].to_broadcast([P, DUO, CROSS]), ALU.not_equal)
                    then(v.tensor_tensor(carry[:, 0], cross[:, :, CROSS - 1], before, ALU.add))
                    then(v.tensor_tensor(carry[:, 1], cross[:, :, CROSS - 1], kt[:, :, 0], ALU.is_equal))
                    then(v.tensor_tensor(carry[:, 0], carry[:, 0], carry[:, 1], ALU.mult))
                    v.tensor_scalar(rec[:, :, REC_CARRY], carry[:, 0], -1.0, None, ALU.add)
                    v.tensor_copy(rec[:, :, REC_PLACE:REC], places.rearrange("p (q t) -> p q t", q=DUO))
                    then(v.tensor_scalar(rec[:, :, REC_PEN + 1:REC_PEN + P], rec[:, :, REC_PEN + 1:REC_PEN + P], -BIG,
                                         None, ALU.mult))
                    v.tensor_scalar(rec[:, :, REC_FIRST:REC_CARRY], rec[:, :, REC_FIRST:REC_CARRY], -BIG, None,
                                    ALU.mult).then_inc(rec_ready, 1)

                def add(i):
                    windows = load_words(nc, g.window_rows[0:1, 0], DVE_ENGINE, RING * i, RING)
                    for k in range(RING):
                        n = RING * i + k
                        at = g.sums[:, bass.ds(windows[k] * UROW, D)]
                        keep = g.keep[:, bass.ds(n, 1)]
                        v.wait_ge(summed, n + 1)
                        need(v, added, n)
                        v.scalar_tensor_tensor(out=at, in0=at, scalar=keep, in1=g.ps[:, k % 2, 0:D],
                                               op0=ALU.mult, op1=ALU.add).then_inc(added, 1)
                        if k == AT_KEYS:
                            edge_keys(i)
                        if k == AT_ENDS:
                            tile_ends(i)
                        if k == AT_RECORD:
                            record(i)

                add(0)
                with v.Fori(1, ROUNDS) as i:
                    add(i)

        end_phase(nc, sems)


class NormTiles:

    def __init__(self, sb, name):
        self.stat = sb(name + "_stat", [P, 2, 6])
        self.mom = sb(name + "_mom", [P, 2, 2])
        self.var = sb(name + "_var", [P, 2])
        self.rstd = sb(name + "_rstd", [P, 2])
        self.bits = sb(name + "_bits", [P, 2], I32)
        self.half = sb(name + "_half", [P, 2])


NORM_SIGNALS = 4 + RSQRT_SIGNALS


def layer_norm(v, y, s, out, done, count):
    for a in range(2):
        d = v.bn_stats(s.stat[:, a, :], y[:, a, :])
    d.then_inc(done, 1)
    need_apart(v, done, count + 1)
    for a in range(2):
        d = v.bn_aggr(s.mom[:, a, :], s.stat[:, a, :])
    d.then_inc(done, 1)
    v.wait_ge(done, count + 2)
    v.tensor_scalar(s.var[:], s.mom[:, :, 1], EPS, None, ALU.add).then_inc(done, 1)
    v.wait_ge(done, count + 3)
    reciprocal_sqrt(v, s.var[:], s.rstd[:], s.bits[:], s.half[:], done, count + 3)
    for a in range(2):
        d = v.tensor_scalar(out[:, a, :], y[:, a, :], s.mom[:, a, 0:1], s.rstd[:, a:a + 1], ALU.subtract, ALU.mult)
    d.then_inc(done, 1)
    v.wait_ge(done, count + NORM_SIGNALS)


def both(vector):
    return vector[:, None, :].to_broadcast([P, 2, D])


STEPS = WINDOWS // 2
assert STEPS % 2 == 1


def real(m):
    return not isinstance(m, int) or 0 <= m < STEPS


def node_steps(eng, emit):
    def turn(i):
        for b in range(2):
            emit(2 * i + b, b, i)

    turn(0)
    turn(1)
    with eng.Fori(2, STEPS // 2) as i:
        turn(i)
    turn(STEPS // 2)
    turn(STEPS // 2 + 1)


def two_windows(dram, n):
    return dram[bass.ds(2 * P * n, 2 * P), :].rearrange("(a p) c -> p a c", a=2)


def gcn_nodes(nc, g):
    with ExitStack() as ctx:
        def sb(name, shape, dt=F32):
            return ctx.enter_context(nc.sbuf_tensor(name, shape, dt))

        def sem(name):
            s = ctx.enter_context(nc.semaphore(name))
            sems.append(s)
            return s

        sems = []
        w = sb("gn_w", [P, 2, D])
        x = sb("gn_x", [P, 2, 2, D])
        a = sb("gn_a", [P, 2, 2, D])
        at = sb("gn_at", [P, 2, 2, P])
        y = sb("gn_y", [P, 2, D])
        scratch = NormTiles(sb, "gn")
        out = sb("gn_out", [P, 2, 2, D])
        w_in = sem("gn_w_in")
        x_in = [sem(f"gn_x_in{b}") for b in range(2)]
        stored = [sem(f"gn_stored{b}") for b in range(2)]
        scaled, turned, copied, mixed, vec = (
            sem("gn_scaled"), sem("gn_turned"), sem("gn_copied"), sem("gn_mixed"), sem("gn_vec"))
        VEC = 1 + NORM_SIGNALS
        ps = g.ps
        with nc.Block() as block:

            @block.sync
            def _(sp):
                sp.dma_start(w[:], g.gcn_w.rearrange("(c k) n -> k c n", c=2)).then_inc(w_in, 16)

                def emit(n, b, i):
                    if real(n):
                        need(sp, vec, VEC * (n - 2) + 1)
                        sp.dma_start(x[:, b], two_windows(g.x_d, n)).then_inc(x_in[b], 16)

                node_steps(sp, emit)

            @block.gpsimd
            def _(pool):
                def emit(n, b, i):
                    if real(n):
                        sums = g.sums[:, bass.ds(2 * UROW * n, 2 * UROW)].rearrange("p (w c) -> p w c", w=2)
                        factor = g.dis[:, bass.ds(2 * n, 2)]
                        need_apart(pool, turned, n - 1)
                        nc.gpsimd.tensor_tensor(a[:, b], sums[:, :, 0:D], factor[:, :, None].to_broadcast([P, 2, D]),
                                                ALU.mult).then_inc(scaled, 1)

                node_steps(pool, emit)

            @block.tensor
            def _(t):
                t.wait_ge(w_in, 16)

                def emit(n, b, i):
                    if real(n):
                        t.wait_ge(scaled, n + 1)
                        need(t, copied, n)
                        for q in range(4):
                            tr = t.transpose(ps[:, 0, q * P:(q + 1) * P], a[:, b, q // 2, (q % 2) * P:(q % 2 + 1) * P], g.ident[:])
                        tr.then_inc(turned, 1)
                        t.wait_ge(copied, n + 1)
                        need(t, vec, VEC * (n - 2) + 1)
                        for k in range(2):
                            for c in range(2):
                                mm = t.matmul(ps[:, 1 + b, k * D:(k + 1) * D], at[:, k, c, :], w[:, c, :], start=c == 0, stop=c == 1)
                        mm.then_inc(mixed, 1)

                node_steps(t, emit)

            @block.scalar
            def _(act):
                def emit(n, b, i):
                    if real(n):
                        act.wait_ge(turned, n + 1)
                        need(act, mixed, n)
                        act.copy(at[:].rearrange("p w c n -> p (w c n)"), ps[:, 0, :]).then_inc(copied, 1)
                    if real(n - 1):
                        act.wait_ge(vec, VEC * n)
                        for dram in (g.x_d, g.x1_d):
                            act.dma_start(two_windows(dram, n - 1), out[:, 1 - b]).then_inc(stored[1 - b], 16)

                node_steps(act, emit)
                act.wait_ge(stored[0], 32 * ((STEPS + 1) // 2))
                act.wait_ge(stored[1], 32 * (STEPS // 2))

            @block.vector
            def _(v):
                def emit(n, b, i):
                    if real(n):
                        v.wait_ge(mixed, n + 1)
                        v.wait_ge(x_in[b], 16 * i + 16)
                        v.tensor_tensor(y[:], ps[:, 1 + b, :].rearrange("p (w c) -> p w c", w=2), x[:, b], ALU.add).then_inc(vec, 1)
                        v.wait_ge(vec, VEC * n + 1)
                        need(v, stored[b], 32 * i)
                        layer_norm(v, y, scratch, out[:, b], vec, VEC * n + 1)

                node_steps(v, emit)

        end_phase(nc, sems)


def project(nc, g, layer):
    with ExitStack() as ctx:
        def sb(name, shape, dt=F32):
            return ctx.enter_context(nc.sbuf_tensor(name, shape, dt))

        def sem(name):
            s = ctx.enter_context(nc.semaphore(name))
            sems.append(s)
            return s

        sems = []
        wk = sb("pj_wk", [P, HEADS, HD])
        wkt = sb("pj_wkt", [HD, HEADS, P])
        we = sb("pj_we", [HD, EDGE_TYPES, HEADS, HD])
        mu = sb("pj_mu", [P, HEADS, EDGE_TYPES])
        w = sb("pj_w", [P, HEADS, PROJ, HD])
        x = sb("pj_x", [P, 2, D])
        xm = sb("pj_xm", [P, 2, HEADS, NODE_TYPES, HD])
        xmt = sb("pj_xmt", [P, 2, HEADS, P])
        ks = sb("pj_k", [P, 2, EDGE_TYPES, HEADS, HD])
        vs = sb("pj_v", [P, 2, HEADS, HD])
        k_in = sem("pj_k_in")
        w_in, kt_turned, kt_copied, w_mixed, mu_scaled, w_ready = (
            sem("pj_w_in"), sem("pj_kt_turned"), sem("pj_kt_copied"), sem("pj_w_mixed"), sem("pj_mu_scaled"),
            sem("pj_w_ready"))
        x_in = [sem(f"pj_x_in{b}") for b in range(2)]
        stored = [sem(f"pj_stored{b}") for b in range(2)]
        masked, turned, copied, mixed, out_v, out_k, out_q = (
            sem("pj_masked"), sem("pj_turned"), sem("pj_copied"), sem("pj_mixed"), sem("pj_out_v"), sem("pj_out_k"),
            sem("pj_out_q"))
        TURNS = WINDOWS // 2
        ps = g.ps
        BANK_HEADS = (range(0, 3), range(3, 6), range(6, 8))
        WIDTH = PROJ * HD

        def bank(b, k):
            return ps[:, 2 + 3 * b + k, 0:len(BANK_HEADS[k]) * WIDTH].rearrange("p (h o e) -> p h o e", o=PROJ, e=HD)

        with nc.Block() as block:

            @block.sync
            def _(sp):
                for t in range(NODE_TYPES):
                    rows = slice(t * HD, (t + 1) * HD)
                    sp.dma_start(wk[rows, :, :], g.w_k[bass.ds(layer, 1), t].rearrange("a h d e -> (a d) h e")).then_inc(k_in, 16)
                sp.dma_start(we[:], g.w_e[bass.ds(layer, 1)].rearrange("a t h m e -> (a m) t h e")).then_inc(k_in, 16)
                sp.dma_start(mu[:].rearrange("p h t -> p (h t)"),
                             g.mu[bass.ds(layer, 1)].rearrange("a h t -> a (h t)")
                             .to_broadcast([P, HEADS * EDGE_TYPES])).then_inc(k_in, 16)

                def store(i):
                    for b in range(2):
                        n = 2 * i + b
                        sp.wait_ge(out_k, n + 1)
                        rows = g.tab_d[:, bass.ds(P * n, P), :].rearrange("t p c -> p t c")
                        sp.dma_start(rows[:, :, 0:D], ks[:, b].rearrange("p t h e -> p t (h e)")).then_inc(stored[b], 16)
                        sp.dma_start(rows[:, :, D:ROW],
                                     vs[:, b].rearrange("p h e -> p (h e)")[:, None, :]
                                     .to_broadcast([P, EDGE_TYPES, D])).then_inc(stored[b], 16)

                store(0)
                with sp.Fori(1, TURNS) as i:
                    store(i)
                for b in range(2):
                    sp.wait_ge(stored[b], 32 * TURNS)

            @block.tensor
            def _(t):
                t.wait_ge(k_in, 16 * (NODE_TYPES + 2))
                for h in range(HEADS):
                    tr = t.transpose(ps[0:HD, h // 4, (h % 4) * P:(h % 4 + 1) * P], wk[:, h, :], g.ident[:])
                tr.then_inc(kt_turned, 1)
                t.wait_ge(kt_copied, 1)
                for h in range(HEADS):
                    mm = t.matmul(ps[:, 2 + h // 4, (h % 4) * EDGE_TYPES * HD:(h % 4 + 1) * EDGE_TYPES * HD],
                                  wkt[:, h, :], we[:, :, h, :], start=True, stop=True)
                mm.then_inc(w_mixed, 1)

                def turn(n, b):
                    t.wait_ge(masked, n + 1)
                    need(t, copied, n)
                    for h in range(HEADS):
                        tr = t.transpose(ps[:, h // 4, (h % 4) * P:(h % 4 + 1) * P],
                                         xm[:, b, h].rearrange("p t d -> p (t d)"), g.ident[:])
                    tr.then_inc(turned, 1)

                def mix(n, b):
                    t.wait_ge(copied, n + 1)
                    need(t, out_v, 3 * (n - 1))
                    need(t, out_k, n - 1)
                    for k, heads in enumerate(BANK_HEADS):
                        for h in heads:
                            mm = t.matmul(bank(b, k)[:, h - heads[0]], xmt[:, b, h, :], w[:, h], start=True, stop=True)
                    mm.then_inc(mixed, 1)

                turn(0, 0)
                t.wait_ge(w_ready, 1)
                t.wait_ge(w_in, 16 * 2 * NODE_TYPES)
                turn(1, 1)
                mix(0, 0)
                with t.Fori(1, TURNS) as i:
                    turn(2 * i, 0)
                    mix(2 * i - 1, 1)
                    turn(2 * i + 1, 1)
                    mix(2 * i, 0)
                mix(WINDOWS - 1, 1)

            @block.scalar
            def _(act):
                def load(i, b):
                    need(act, masked, 2 * i + b - 1)
                    act.dma_start(x[:, b, :], g.x_d[bass.ds(P * (2 * i + b), P), :]).then_inc(x_in[b], 16)

                load(0, 0)
                load(0, 1)
                for t in range(NODE_TYPES):
                    rows = slice(t * HD, (t + 1) * HD)
                    for dram, dest in ((g.w_q, w[rows, :, 0, :]), (g.w_v, w[rows, :, 1, :])):
                        act.dma_start(dest, dram[bass.ds(layer, 1), t].rearrange("a h d e -> (a d) h e")).then_inc(w_in, 16)
                act.wait_ge(kt_turned, 1)
                act.copy(wkt[:].rearrange("p (b h) n -> p b (h n)", b=2), ps[0:HD, 0:2, :]).then_inc(kt_copied, 1)

                def copy(n, b):
                    act.wait_ge(turned, n + 1)
                    need(act, mixed, n - 1)
                    act.copy(xmt[:, b].rearrange("p (k h) n -> p k (h n)", k=2), ps[:, 0:2, :]).then_inc(copied, 1)

                def out(i, b):
                    n = 2 * i + b
                    act.wait_ge(mixed, n + 1)
                    need(act, stored[b], 32 * i)
                    for k, heads in enumerate(BANK_HEADS):
                        act.copy(vs[:, b, heads[0]:heads[-1] + 1, :], bank(b, k)[:, :, 1, :]).then_inc(out_v, 1)

                copy(0, 0)
                load(1, 0)
                copy(1, 1)
                load(1, 1)
                out(0, 0)

                def turn(i, more=True):
                    copy(2 * i, 0)
                    if more:
                        load(i + 1, 0)
                    out(i - 1, 1)
                    copy(2 * i + 1, 1)
                    if more:
                        load(i + 1, 1)
                    out(i, 0)

                with act.Fori(1, TURNS - 1) as i:
                    turn(i)
                turn(TURNS - 1, more=False)
                out(TURNS - 1, 1)

            @block.gpsimd
            def _(pool):
                def mask(i, b):
                    n = 2 * i + b
                    shape = [P, HEADS, NODE_TYPES, HD]
                    types = g.type_hot[:, bass.ds(n, 1), :][:, :, :, None].to_broadcast(shape)
                    pool.wait_ge(x_in[b], 16 * i + 16)
                    need(pool, turned, n - 1)
                    nc.gpsimd.tensor_tensor(xm[:, b],
                                    x[:, b, :].rearrange("p (h d) -> p h d", h=HEADS)[:, :, None, :].to_broadcast(shape),
                                    types, ALU.mult).then_inc(masked, 1)

                mask(0, 0)
                mask(0, 1)
                with pool.Fori(1, TURNS) as i:
                    mask(i, 0)
                    mask(i, 1)

            @block.vector
            def _(v):
                v.wait_ge(k_in, 16 * (NODE_TYPES + 2))
                v.tensor_scalar(mu[:], mu[:], float(HD) ** -0.5, None, ALU.mult).then_inc(mu_scaled, 1)

                def out(i, b):
                    n = 2 * i + b
                    need(v, stored[b], 32 * i)
                    for k, heads in enumerate(BANK_HEADS):
                        q_row = g.sums[:, bass.ds(UROW * (n + 1) + heads[0] * HD, len(heads) * HD)]
                        v.wait_ge(out_v, 3 * n + k + 1)
                        v.tensor_copy(ks[:, b, :, heads[0]:heads[-1] + 1, :].rearrange("p t h e -> p h t e"),
                                      bank(b, k)[:, :, 2:PROJ, :])
                        d = v.tensor_copy(q_row.rearrange("p (h e) -> p h e", e=HD), bank(b, k)[:, :, 0, :])
                    d.then_inc(out_k, 1)

                v.wait_ge(w_mixed, 1)
                v.wait_ge(mu_scaled, 1)
                for half in range(2):
                    shape = [P, 4, EDGE_TYPES, HD]
                    d = v.tensor_tensor(w[:, 4 * half:4 * half + 4, 2:PROJ, :],
                                        ps[:, 2 + half, 0:4 * EDGE_TYPES * HD].rearrange("p (h t e) -> p h t e", h=4, t=EDGE_TYPES),
                                        mu[:, 4 * half:4 * half + 4, :, None].to_broadcast(shape), ALU.mult)
                d.then_inc(w_ready, 1)
                with v.Fori(1, TURNS) as i:
                    out(i - 1, 0)
                    out(i - 1, 1)
                out(TURNS - 1, 0)
                out(TURNS - 1, 1)

        end_phase(nc, sems)


LAG_COPY = 1
LAG_SCORE = 2
LAG_WEIGH = 13
LAG_SUM = 14
LAG_ADD = 15
SPLIT = 6
SOFT_TURN, SOFT_CROSS, SOFT_OUT, SOFT_WEIGHTS, SOFT_RESCALE = 2, 3, 4, 5, 7


HC = HIDDEN // P


class NodeWeights:

    def __init__(self, nc, ctx):
        def sb(name, shape):
            return ctx.enter_context(nc.sbuf_tensor(name, shape, F32))

        self.wo = sb("nw_wo", [P, 2, D])
        self.w1 = sb("nw_w1", [P, 2, HIDDEN])
        self.w2 = sb("nw_w2", [P, HC, D])
        self.b1_row = sb("nw_b1_row", [HC, P])
        self.rows = sb("nw_rows", [P, 6, D])
        self.loaded = ctx.enter_context(nc.semaphore("nw_loaded"))


def attention_edges(nc, g, layer, nw):
    with ExitStack() as ctx:
        def sb(name, shape, dt=F32):
            return ctx.enter_context(nc.sbuf_tensor(name, shape, dt))

        def sem(name):
            s = ctx.enter_context(nc.semaphore(name))
            sems.append(s)
            return s

        sems = []
        kv = sb("at_kv", [P, 2 * RING, SLOT])
        hot = sb("at_hot", [P, RING, 2, P])
        hot_t = sb("at_hot_t", [P, 2, 2, P])
        dist = sb("at_dist", [P, 2, 2, P])
        idx = sb("at_idx", [P, 2, TILES], I32)
        rec = sb("at_rec", [P, 2, REC])
        score = sb("at_score", [P, 2, TILES, HEADS])
        floor = sb("at_floor", [P, P])
        run = sb("at_run", [P, P])
        top = sb("at_top", [P, P])
        ends = sb("at_ends", [P, CROSS])
        seen = sb("at_seen", [P, 2, CROSS])
        ends_max = sb("at_ends_max", [P, 2, 2])
        fall = sb("at_fall", [P, 1])
        fall_row = sb("at_fall_row", [P, P])
        top_first = sb("at_top_first", [P, P])
        top_all = sb("at_top_all", [P, P])
        fade = sb("at_fade", [P, 2, HEADS])
        idx_in = [sem(f"at_idx_in{b}") for b in range(2)]
        rec_in = [sem(f"at_rec_in{b}") for b in range(2)]
        landed = g.landed
        before = PASS_LANDED * (layer + 1)
        weighed_too = sem("at_weighed_too")
        (dist_ready, hot_ready, turned, copied, q_ready, multiplied, scored, weighed, summed, added) = (
            sem("at_dist_ready"), sem("at_hot_ready"), sem("at_turned"), sem("at_copied"), sem("at_q_ready"),
            sem("at_multiplied"), sem("at_scored"), sem("at_weighed"), sem("at_summed"), sem("at_added"))
        (scores_turned, soft, ends_ready, crossed, tops_ready, lowered, faded, weights_ready, rescaled) = (
            sem("at_scores_turned"), sem("at_soft"), sem("at_ends_ready"), sem("at_crossed"),
            sem("at_tops_ready"), sem("at_lowered"), sem("at_faded"),
            sem("at_weights_ready"), sem("at_rescaled"))
        ps = g.ps
        TURN_BANK, Q_BANK, SUM_BANK, SOFT_BANK = 0, 2, 4, 6
        SCORES_T, ENDS_AT, FADE_AT, LESS = slice(0, P), slice(P, P + CROSS), slice(176, 176 + HEADS), slice(2 * P, 3 * P)

        def steps(i, emit):
            for k in range(RING):
                def at(lag, k=k):
                    n = RING * i + (k - lag)
                    if isinstance(n, int) and not 0 <= n < PAIRS:
                        return None
                    return n, (k - lag) % RING, i + (k - lag) // RING
                emit(k, at)

        def soft_block(i, k, stage):
            if k % BLOCK != stage:
                return None
            b = 2 * i + k // BLOCK - 1
            if isinstance(b, int) and not 0 <= b < BLOCKS:
                return None
            return b, (k // BLOCK - 1) % 2

        with nc.Block() as block:

            @block.sync
            def _(sp):
                def load_block(i, b):
                    blk = 2 * i + b
                    need(sp, tops_ready, blk - 1)
                    sp.dma_start(idx[:, b, :], g.idx_d[1, bass.ds(blk, 1)].rearrange("b p t -> (b p) t")).then_inc(idx_in[b], 16)
                    sp.dma_start(rec[:, b, :], g.rec_d[bass.ds(blk, 1)].rearrange("b p r -> (b p) r")).then_inc(rec_in[b], 16)

                load_block(0, 0)
                load_block(0, 1)
                sp.dma_start(nw.wo[:], g.wo[bass.ds(layer, 1)].rearrange("a (c k) n -> k (a c) n", c=2)).then_inc(nw.loaded, 16)
                for k, dram in enumerate((g.bo, g.ln1_g, g.ln1_b, g.b2, g.ln2_g, g.ln2_b)):
                    sp.dma_start(nw.rows[:, k, :], dram[bass.ds(layer, 1), :].to_broadcast([P, D])).then_inc(nw.loaded, 16)
                sp.dma_start(nw.b1_row[:], g.b1[bass.ds(layer, 1)].rearrange("a (c k) -> (a c) k", c=HC)).then_inc(nw.loaded, 16)
                sp.dma_start(nw.w1[:], g.w1[bass.ds(layer, 1)].rearrange("a (c k) n -> k (a c) n", c=2)).then_inc(nw.loaded, 16)
                sp.dma_start(nw.w2[:], g.w2[bass.ds(layer, 1)].rearrange("a (c k) n -> k (a c) n", c=HC)).then_inc(nw.loaded, 16)
                with sp.Fori(1, ROUNDS) as i:
                    load_block(i, 0)
                    load_block(i, 1)

            @block.gpsimd
            def _(pool):
                def gather(i):
                    for k in range(RING):
                        b, u = divmod(k, BLOCK)
                        if u == 0:
                            need_apart(pool, idx_in[b], 16 * i + 16)
                        need_apart(pool, summed, RING * i + k - RING + 1)
                        for j in range(2):
                            nc.gpsimd.indirect_dma_start(
                                kv[:, 2 * k + j, 0:ROW], None, g.tab_d.rearrange("t n c -> (t n) c"),
                                bass.IndirectOffsetOnAxis(idx[:, b, 2 * u + j:2 * u + j + 1], 0)).then_inc(landed[k], 16)

                gather(0)
                with pool.Fori(1, ROUNDS) as i:
                    gather(i)

            @block.scalar
            def _(act):
                def emit(k, at, i):
                    if now := at(0):
                        n, slot, turn = now
                        b, u = divmod(slot, BLOCK)
                        if u == 0:
                            act.wait_ge(rec_in[b], 16 * turn + 16)
                        for j in range(2):
                            d = act.activation(dist[:, slot % 2, j, :], g.iota[:], ACT.Abs,
                                               bias=rec[:, b, REC_PLACE + 2 * u + j:REC_PLACE + 2 * u + j + 1])
                        d.then_inc(dist_ready, 1)
                    if now := at(LAG_COPY):
                        n, slot, turn = now
                        act.wait_ge(turned, n + 1)
                        need(act, q_ready, n - 1)
                        act.copy(hot_t[:, slot % 2].rearrange("p j e -> p (j e)"),
                                 ps[:, TURN_BANK + slot % 2, 0:GROUP]).then_inc(copied, 1)
                    if now := at(0):
                        n, slot, turn = now
                        need(act, summed, n - RING + 1)
                        act.wait_ge(dist_ready, n + 1)
                        act.activation(hot[:, slot], dist[:, slot % 2], ACT.Relu, bias=1.0, scale=-1.0).then_inc(hot_ready, 1)
                    if blk := soft_block(i, k, SOFT_WEIGHTS):
                        b, par = blk
                        act.wait_ge(lowered, b + 1)
                        need(act, rescaled, b - 1)
                        act.activation(fade[:, par, :], ps[:, SOFT_BANK + par, FADE_AT], ACT.Exp).then_inc(faded, 1)
                        act.activation(kv[:, TILES * par:TILES * (par + 1), ROW:SLOT],
                                       ps[:, SOFT_BANK + par, LESS].rearrange("p (t h) -> p t h", h=HEADS),
                                       ACT.Exp).then_inc(weights_ready, 1)
                    if now := at(LAG_WEIGH):
                        n, slot, turn = now
                        if slot % BLOCK == 0:
                            act.wait_ge(weights_ready, 2 * turn + slot // BLOCK + 1)
                        for j in range(2):
                            for h in range(SPLIT, HEADS):
                                values = kv[:, 2 * slot + j, D + h * HD:D + (h + 1) * HD]
                                d = act.activation(values, values, ACT.Copy,
                                                   scale=kv[:, 2 * slot + j, ROW + h:ROW + h + 1])
                        d.then_inc(weighed_too, 1)

                def turn(i):
                    steps(i, lambda k, at: emit(k, at, i))

                turn(0)
                with act.Fori(1, ROUNDS) as i:
                    turn(i)
                turn(ROUNDS)

            @block.tensor
            def _(t):
                def emit(k, at, i, windows):
                    if k == 0:
                        windows.extend(load_words(nc, g.window_rows[0:1, g.shifts.index(LAG_COPY)], PE_ENGINE, RING * i, RING))
                    if now := at(LAG_COPY):
                        n, slot, turn = now
                        q_rows = g.sums[:, bass.ds(windows[k] * UROW + UROW, D)]
                        t.wait_ge(copied, n + 1)
                        need(t, multiplied, n - 1)
                        for j in range(2):
                            mm = t.matmul(ps[:, Q_BANK + slot % 2, j * D:(j + 1) * D], hot_t[:, slot % 2, j, :], q_rows,
                                          start=True, stop=True)
                        mm.then_inc(q_ready, 1)
                    if now := at(0):
                        n, slot, turn = now
                        t.wait_ge(hot_ready, n + 1)
                        need(t, copied, n - 1)
                        for j in range(2):
                            tr = t.transpose(ps[:, TURN_BANK + slot % 2, j * P:(j + 1) * P], hot[:, slot, j, :], g.ident[:])
                        tr.then_inc(turned, 1)
                    if blk := soft_block(i, k, SOFT_TURN):
                        b, par = blk
                        t.wait_ge(scored, BLOCK * (b + 1))
                        need(t, weights_ready, b - 1)
                        t.transpose(ps[:, SOFT_BANK + par, SCORES_T], score[:, par].rearrange("p t h -> p (t h)"),
                                    g.ident[:]).then_inc(scores_turned, 1)
                    if blk := soft_block(i, k, SOFT_CROSS):
                        b, par = blk
                        t.wait_ge(ends_ready, b + 1)
                        t.matmul(ps[:, SOFT_BANK + par, ENDS_AT], g.same_head[:], ends[:], start=True, stop=True).then_inc(crossed, 1)
                    if blk := soft_block(i, k, SOFT_OUT):
                        b, par = blk
                        t.wait_ge(tops_ready, b + 1)
                        t.matmul(ps[:, SOFT_BANK + par, FADE_AT], fall_row[:], g.ident[:, 0:HEADS], start=True, stop=True)
                        t.matmul(ps[:, SOFT_BANK + par, LESS], g.ident[:], score[:, par].rearrange("p t h -> p (t h)"),
                                 start=True, stop=False)
                        t.matmul(ps[:, SOFT_BANK + par, LESS], top_all[:], g.minus_ident[:],
                                 start=False, stop=True).then_inc(lowered, 1)
                    if now := at(LAG_SUM):
                        n, slot, turn = now
                        t.wait_ge(weighed, n + 1)
                        t.wait_ge(weighed_too, n + 1)
                        need(t, added, n - 1)
                        for j in range(2):
                            mm = t.matmul(ps[:, SUM_BANK + slot % 2, 0:UROW], hot[:, slot, j, :], kv[:, 2 * slot + j, D:SLOT],
                                          start=j == 0, stop=j == 1)
                        mm.then_inc(summed, 1)

                def turn(i):
                    windows = []
                    steps(i, lambda k, at: emit(k, at, i, windows))

                turn(0)
                with t.Fori(1, ROUNDS) as i:
                    turn(i)
                turn(ROUNDS)

            @block.vector
            def _(v):
                def emit(k, at, i, windows):
                    score_now, weigh_now, add_now = at(LAG_SCORE), at(LAG_WEIGH), at(LAG_ADD)
                    maxima, across = soft_block(i, k, SOFT_TURN), soft_block(i, k, SOFT_CROSS)
                    if score_now:
                        n, slot, turn = score_now
                        v.wait_ge(q_ready, n + 1)
                        v.wait_ge(landed[slot], before + 32 * turn + 32)
                        keys = kv[:, 2 * slot:2 * slot + 2, 0:D]
                        v.tensor_tensor(keys, ps[:, Q_BANK + slot % 2, :].rearrange("p (j c) -> p j c", j=2), keys,
                                        ALU.mult).then_inc(multiplied, 1)
                    if across:
                        b, par = across
                        v.wait_ge(crossed, b + 1)
                        need(v, lowered, b)
                        shape = [P, 2, CROSS]
                        v.tensor_tensor(seen[:], ps[:, SOFT_BANK + par, ENDS_AT][:, None, :].to_broadcast(shape),
                                        rec[:, par, REC_CROSS:REC_CARRY].rearrange("p (k c) -> p k c", k=2),
                                        ALU.add).then_inc(soft, 1)
                    if weigh_now:
                        n, slot, turn = weigh_now
                        if slot % BLOCK == 0:
                            v.wait_ge(weights_ready, 2 * turn + slot // BLOCK + 1)
                        shape = [P, 2, SPLIT, HD]
                        values = kv[:, 2 * slot:2 * slot + 2, D:D + SPLIT * HD].rearrange("p j (h e) -> p j h e", h=SPLIT)
                        v.tensor_tensor(values, values,
                                        kv[:, 2 * slot:2 * slot + 2, ROW:ROW + SPLIT][:, :, :, None].to_broadcast(shape),
                                        ALU.mult).then_inc(weighed, 1)
                    if maxima:
                        b, par = maxima
                        v.wait_ge(scores_turned, b + 1)
                        v.wait_ge(rec_in[par], 8 * (b - par) + 16)
                        need(v, crossed, b)
                        v.tensor_tensor(ends[:, CROSS - 1:CROSS], g.tile_hot[:, TILES - 1:TILES],
                                        ends_max[:, 1 - par, 1:2], ALU.mult)
                        v.tensor_scalar(floor[:], ps[:, SOFT_BANK + par, SCORES_T], FLOOR, None, ALU.max).then_inc(soft, 1)
                    if across:
                        b, par = across
                        v.wait_ge(soft, 7 * b + 5)
                        v.tensor_reduce(ends_max[:, par, :], seen[:], AX.X, ALU.max).then_inc(soft, 1)
                    if blk := soft_block(i, k, SOFT_RESCALE):
                        b, par = blk
                        values = g.sums[:, bass.ds(windows[k - 1] * UROW, D)].rearrange("p (h e) -> p h e", h=HEADS)
                        weights = g.sums[:, bass.ds(windows[k - 1] * UROW + D, HEADS)]
                        v.wait_ge(faded, b + 1)
                        need(v, added, BLOCK * b)
                        v.tensor_tensor(values, values, fade[:, par, :, None].to_broadcast([P, HEADS, HD]), ALU.mult)
                        v.tensor_tensor(weights, weights, fade[:, par, :], ALU.mult).then_inc(rescaled, 1)
                    if score_now:
                        n, slot, turn = score_now
                        par, u = divmod(slot, BLOCK)
                        v.wait_ge(multiplied, n + 1)
                        if u == 0:
                            need(v, lowered, 2 * turn + par - 1)
                        v.tensor_reduce(score[:, par, 2 * u:2 * u + 2, :],
                                        kv[:, 2 * slot:2 * slot + 2, 0:D].rearrange("p j (h e) -> p j h e", h=HEADS),
                                        AX.X, ALU.add).then_inc(scored, 1)
                    if k == 0:
                        windows.extend(load_words(nc, g.window_rows[0:1, g.shifts.index(LAG_ADD)], DVE_ENGINE, RING * i, RING))
                    if maxima:
                        b, par = maxima
                        v.wait_ge(soft, 7 * b + 2)
                        v.tensor_tensor_scan(run[:], rec[:, par, REC_PEN:REC_PEN + P], floor[:], 0.0, ALU.add,
                                             ALU.max).then_inc(soft, 1)
                    if across:
                        b, par = across
                        v.wait_ge(soft, 7 * b + 6)
                        v.tensor_tensor(fall[:], ps[:, SOFT_BANK + par, P + CROSS - 1:P + CROSS], ends_max[:, par, 0:1],
                                        ALU.subtract).then_inc(soft, 1)
                        v.scalar_tensor_tensor(out=top_first[:], in0=rec[:, par, REC_FIRST:REC_FIRST + P],
                                               scalar=ends_max[:, par, 0:1], in1=top[:], op0=ALU.add,
                                               op1=ALU.max).then_inc(soft, 1)
                    if add_now:
                        n, slot, turn = add_now
                        rows = g.sums[:, bass.ds(windows[k] * UROW, UROW)]
                        keep = g.keep[:, bass.ds(n, 1)]
                        v.wait_ge(summed, n + 1)
                        need(v, added, n)
                        if slot % BLOCK == 0:
                            v.wait_ge(rescaled, 2 * turn + slot // BLOCK + 1)
                        v.scalar_tensor_tensor(out=rows, in0=rows, scalar=keep,
                                               in1=ps[:, SUM_BANK + slot % 2, 0:UROW], op0=ALU.mult, op1=ALU.add).then_inc(added, 1)
                    if maxima:
                        b, par = maxima
                        v.wait_ge(soft, 7 * b + 3)
                        v.tensor_tensor_scan(top[:, ::-1], rec[:, par, REC_PEN + P:REC_PEN:-1], run[:, ::-1], 0.0,
                                             ALU.add, ALU.max).then_inc(soft, 1)
                        v.wait_ge(soft, 7 * b + 4)
                        shape = [P, 2, TILES]
                        v.tensor_tensor(ends[:, 0:2 * TILES].rearrange("p (k t) -> p k t", k=2),
                                        g.tile_hot[:, None, :].to_broadcast(shape),
                                        top[:, ::P - 1][:, :, None].to_broadcast(shape), ALU.mult).then_inc(ends_ready, 1)
                    if across:
                        b, par = across
                        v.wait_ge(soft, 7 * b + 7)
                        v.tensor_scalar(fall_row[:], g.iota[:], rec[:, par, REC_CARRY:REC_CARRY + 1], fall[:],
                                        ALU.is_equal, ALU.mult)
                        v.wait_ge(soft, 7 * b + 8)
                        v.scalar_tensor_tensor(out=top_all[:], in0=rec[:, par, REC_LAST:REC_LAST + P],
                                               scalar=ends_max[:, par, 1:2], in1=top_first[:], op0=ALU.add,
                                               op1=ALU.max).then_inc(tops_ready, 1)

                def turn(i):
                    windows = []
                    steps(i, lambda k, at: emit(k, at, i, windows))

                v.memset(ends_max[:], 0.0).then_inc(soft, 1)
                v.wait_ge(soft, 1)
                turn(0)
                with v.Fori(1, ROUNDS) as i:
                    turn(i)
                turn(ROUNDS)

        end_phase(nc, sems)


def attention_nodes(nc, g, layer, nw):
    with ExitStack() as ctx:
        def sb(name, shape, dt=F32):
            return ctx.enter_context(nc.sbuf_tensor(name, shape, dt))

        def sem(name):
            s = ctx.enter_context(nc.semaphore(name))
            sems.append(s)
            return s

        sems = []
        wo, w1, w2, b1_row, rows, w_in = nw.wo, nw.w1, nw.w2, nw.b1_row, nw.rows, nw.loaded
        sems.append(w_in)
        b1 = sb("an_b1", [P, HC])
        x = sb("an_x", [P, 2, 2, D])
        some = sb("an_some", [P, 2, 2, HEADS])
        part = sb("an_part", [P, 2, 2, HEADS])
        a = sb("an_a", [P, 2, 2, D])
        at = sb("an_at", [P, 2, 2, P])
        xb = sb("an_xb", [P, 2, 2, D])
        y = sb("an_y", [P, 2, D])
        yn = sb("an_yn", [P, 2, D])
        yg = sb("an_yg", [P, 2, D])
        zn = sb("an_zn", [P, 2, D])
        zg = sb("an_zg", [P, 2, D])
        scratch = NormTiles(sb, "an")
        x1 = sb("an_x1", [P, 2, 2, D])
        x1b = sb("an_x1b", [P, 2, 2, D])
        x1t = sb("an_x1t", [P, 2, 2, P])
        ht = sb("an_ht", [P, HC, 2 * P])
        out = sb("an_out", [P, 2, 2, D])
        x_in = [sem(f"an_x_in{b}") for b in range(2)]
        stored = [sem(f"an_stored{b}") for b in range(2)]
        (b1_turned, b1_copied, shared, averaged, a_turned, a_copied, attended, vec1, x1_ready, x1_turned, x1_copied,
         hidden, activated, fed, vec2, normed, x_biased, x1_biased, gained) = (
            sem("an_b1_turned"), sem("an_b1_copied"), sem("an_shared"), sem("an_averaged"), sem("an_a_turned"),
            sem("an_a_copied"), sem("an_attended"), sem("an_vec1"), sem("an_x1_ready"), sem("an_x1_turned"),
            sem("an_x1_copied"), sem("an_hidden"), sem("an_activated"), sem("an_fed"), sem("an_vec2"), sem("an_normed"),
            sem("an_x_biased"), sem("an_x1_biased"), sem("an_gained"))
        CHAIN1 = 2 + NORM_SIGNALS
        CHAIN2 = 1 + NORM_SIGNALS
        BO, LN1_G, LN1_B, B2, LN2_G, LN2_B = range(6)
        ps = g.ps

        with nc.Block() as block:

            @block.sync
            def _(sp):
                def emit(n, b, i):
                    if real(n):
                        need(sp, x_biased, n - 1)
                        sp.dma_start(x[:, b], g.x_d[bass.ds(2 * P * n, 2 * P), :].rearrange("(a p) c -> p a c", a=2)).then_inc(x_in[b], 16)
                    if real(n - 2):
                        sp.wait_ge(normed, n - 1)
                        sp.dma_start(g.x_d[bass.ds(2 * P * (n - 2), 2 * P), :].rearrange("(a p) c -> p a c", a=2),
                                     out[:, b]).then_inc(stored[b], 16)

                node_steps(sp, emit)
                sp.wait_ge(stored[0], 16 * ((STEPS + 1) // 2))
                sp.wait_ge(stored[1], 16 * (STEPS // 2))

            @block.tensor
            def _(t):
                t.wait_ge(w_in, 16 * 10)
                t.transpose(ps[:, 2, 0:HC], b1_row[:], g.ident[0:HC, 0:HC]).then_inc(b1_turned, 1)
                t.wait_ge(b1_copied, 1)

                def emit(n, b, i):
                    if real(n):
                        t.wait_ge(averaged, n + 1)
                        need(t, a_copied, n)
                        for q in range(4):
                            tr = t.transpose(ps[:, 0, q * P:(q + 1) * P], a[:, b, q // 2, (q % 2) * P:(q % 2 + 1) * P], g.ident[:])
                        tr.then_inc(a_turned, 1)
                    if real(n - 2):
                        t.wait_ge(activated, HC * (n - 1))
                        need(t, vec2, CHAIN2 * (n - 3) + 1)
                        for w in range(2):
                            for c in range(HC):
                                mm = t.matmul(ps[:, 7, w * D:(w + 1) * D], ht[:, c, w * P:(w + 1) * P], w2[:, c, :],
                                              start=c == 0, stop=c == HC - 1)
                        mm.then_inc(fed, 1)
                    if real(n - 1):
                        t.wait_ge(x1_ready, n)
                        need(t, x1_copied, n - 1)
                        for c in range(2):
                            for w in range(2):
                                q = 2 * c + w
                                tr = t.transpose(ps[:, 2, q * P:(q + 1) * P], x1[:, 1 - b, w, c * P:(c + 1) * P], g.ident[:])
                        tr.then_inc(x1_turned, 1)
                    if real(n):
                        t.wait_ge(a_copied, n + 1)
                        need(t, vec1, CHAIN1 * (n - 1) + 1)
                        for w in range(2):
                            for c in range(2):
                                mm = t.matmul(ps[:, 1, w * D:(w + 1) * D], at[:, w, c, :], wo[:, c, :], start=c == 0, stop=c == 1)
                        mm.then_inc(attended, 1)
                    if real(n - 1):
                        t.wait_ge(x1_copied, n)
                        for f in range(HC):
                            if f % 2 == 0:
                                need(t, activated, HC * (n - 2) + f + 2)
                            for c in range(2):
                                mm = t.matmul(ps[:, 3 + f // 2, (f % 2) * 2 * P:(f % 2 + 1) * 2 * P],
                                              w1[:, c, f * P:(f + 1) * P], x1t[:, c].rearrange("p w n -> p (w n)"),
                                              start=c == 0, stop=c == 1)
                            mm.then_inc(hidden, 1)

                node_steps(t, emit)

            @block.scalar
            def _(act):
                act.wait_ge(b1_turned, 1)
                act.copy(b1[:], ps[:, 2, 0:HC]).then_inc(b1_copied, 1)
                act.wait_ge(b1_copied, 1)

                def emit(n, b, i):
                    if real(n):
                        act.wait_ge(a_turned, n + 1)
                        need(act, attended, n)
                        act.copy(at[:].rearrange("p w c n -> p (w c n)"), ps[:, 0, :]).then_inc(a_copied, 1)
                    if real(n - 1):
                        act.wait_ge(x1_turned, n)
                        need(act, hidden, HC * (n - 1))
                        act.copy(x1t[:].rearrange("p c w n -> p (c w n)"), ps[:, 2, :]).then_inc(x1_copied, 1)
                        need(act, fed, n - 1)
                        for f in range(HC):
                            act.wait_ge(hidden, HC * (n - 1) + (f | 1) + 1)
                            act.activation(ht[:, f, :], ps[:, 3 + f // 2, (f % 2) * 2 * P:(f % 2 + 1) * 2 * P], ACT.Gelu,
                                           bias=b1[:, f:f + 1]).then_inc(activated, 1)

                node_steps(act, emit)

            @block.gpsimd
            def _(pool):
                pool.wait_ge(w_in, 16 * 10)

                def emit(n, b, i):
                    if real(n):
                        pool.wait_ge(x_in[b], 16 * i + 16)
                        need(pool, vec1, CHAIN1 * (n - 2) + 1)
                        nc.gpsimd.tensor_tensor(xb[:, b], x[:, b], both(rows[:, BO]), ALU.add).then_inc(x_biased, 1)
                    if real(n - 2):
                        need(pool, normed, n - 2)
                        pool.wait_ge(vec2, CHAIN2 * (n - 1))
                        nc.gpsimd.tensor_tensor(zg[:], zn[:], both(rows[:, LN2_G]), ALU.mult).then_inc(gained, 1)
                        pool.wait_ge(gained, n - 1)
                        need(pool, stored[b], 16 * (i - 1))
                        nc.gpsimd.tensor_tensor(out[:, b], zg[:], both(rows[:, LN2_B]), ALU.add).then_inc(normed, 1)
                    if real(n):
                        pool.wait_ge(x1_ready, n + 1)
                        nc.gpsimd.tensor_tensor(x1b[:, b], x1[:, b], both(rows[:, B2]), ALU.add).then_inc(x1_biased, 1)

                node_steps(pool, emit)

            @block.vector
            def _(v):
                v.wait_ge(w_in, 16 * 10)

                def average(n, b):
                    sums = g.sums[:, bass.ds(2 * UROW * n, 2 * UROW)].rearrange("p (w c) -> p w c", w=2)
                    need(v, a_turned, n - 1)
                    v.tensor_scalar(some[:, b], sums[:, :, D:UROW], SOFT_EPS, None, ALU.add).then_inc(shared, 1)
                    v.wait_ge(shared, 2 * n + 1)
                    v.reciprocal(part[:, b], some[:, b]).then_inc(shared, 1)
                    v.wait_ge(shared, 2 * n + 2)
                    v.tensor_tensor(a[:, b].rearrange("p w (h e) -> p w h e", h=HEADS),
                                    sums[:, :, 0:D].rearrange("p w (h e) -> p w h e", h=HEADS),
                                    part[:, b, :, :, None].to_broadcast([P, 2, HEADS, HD]), ALU.mult).then_inc(averaged, 1)

                average(0, 0)

                def emit(n, b, i):
                    if real(n + 1):
                        average(n + 1, 1 - b)
                    if real(n - 2):
                        v.wait_ge(fed, n - 1)
                        v.wait_ge(x1_biased, n - 1)
                        count = CHAIN2 * (n - 2)
                        v.tensor_tensor(y[:], ps[:, 7, :].rearrange("p (w c) -> p w c", w=2), x1b[:, b], ALU.add).then_inc(vec2, 1)
                        v.wait_ge(vec2, count + 1)
                        need(v, gained, n - 2)
                        layer_norm(v, y, scratch, zn, vec2, count + 1)
                    if real(n):
                        v.wait_ge(attended, n + 1)
                        v.wait_ge(x_biased, n + 1)
                        count = CHAIN1 * n
                        v.tensor_tensor(y[:], ps[:, 1, :].rearrange("p (w c) -> p w c", w=2), xb[:, b], ALU.add).then_inc(vec1, 1)
                        v.wait_ge(vec1, count + 1)
                        layer_norm(v, y, scratch, yn, vec1, count + 1)
                        v.tensor_tensor(yg[:], yn[:], both(rows[:, LN1_G]), ALU.mult).then_inc(vec1, 1)
                        v.wait_ge(vec1, count + CHAIN1)
                        v.tensor_tensor(x1[:, b], yg[:], both(rows[:, LN1_B]), ALU.add).then_inc(x1_ready, 1)

                node_steps(v, emit)

        end_phase(nc, sems)


def last_norms(nc, g):
    with ExitStack() as ctx:
        def sb(name, shape, dt=F32):
            return ctx.enter_context(nc.sbuf_tensor(name, shape, dt))

        def sem(name):
            s = ctx.enter_context(nc.semaphore(name))
            sems.append(s)
            return s

        sems = []
        LAG = 2
        rows = sb("ln_rows", [P, 2, D])
        x = sb("ln_x", [P, 2, 2, D])
        x1 = sb("ln_x1", [P, 2, 2, D])
        yn = sb("ln_yn", [P, 2, D])
        yg = sb("ln_yg", [P, 2, D])
        x1b = sb("ln_x1b", [P, 2, D])
        z = sb("ln_z", [P, 2, 2, D])
        stat = sb("ln_stat", [P, 4, 6])
        mom = sb("ln_mom", [P, 4, 2])
        var = sb("ln_var", [P, 4])
        bits = sb("ln_bits", [P, 4], I32)
        half = sb("ln_half", [P, 4])
        rstd = sb("ln_rstd", [P, 2, 4])
        shift = sb("ln_shift", [P, 2, 4])
        out = sb("ln_out", [P, 2, 2, D])
        w_in, vec, normed, gained, shifted, summed, final = (
            sem("ln_w_in"), sem("ln_vec"), sem("ln_normed"), sem("ln_gained"), sem("ln_shifted"), sem("ln_summed"),
            sem("ln_final"))
        x_in = [sem(f"ln_x_in{b}") for b in range(2)]
        x1_in = [sem(f"ln_x1_in{b}") for b in range(2)]
        stored = [sem(f"ln_stored{b}") for b in range(2)]
        VEC = 4 + RSQRT_SIGNALS
        left = N - 2 * P * (STEPS - 1)
        assert left <= P

        def alive(n):
            return not isinstance(n, int) or n < STEPS + LAG

        with nc.Block() as block:

            @block.sync
            def _(sp):
                sp.dma_start(rows[:, 0, :], g.out_g.rearrange("(a d) -> a d", a=1).to_broadcast([P, D])).then_inc(w_in, 16)
                sp.dma_start(rows[:, 1, :], g.out_b.rearrange("(a d) -> a d", a=1).to_broadcast([P, D])).then_inc(w_in, 16)

                def emit(n, b, i):
                    if real(n):
                        need(sp, normed, n - 1)
                        sp.dma_start(x[:, b], two_windows(g.x_d, n)).then_inc(x_in[b], 16)
                        need(sp, shifted, n - 1)
                        sp.dma_start(x1[:, b], two_windows(g.x1_d, n)).then_inc(x1_in[b], 16)

                node_steps(sp, emit)

            @block.vector
            def _(v):
                for k in range(4):
                    d = v.bn_stats(stat[:, k, :], g.zeros[:])
                d.then_inc(vec, 1)
                v.wait_ge(vec, 1)

                def emit(n, b, i):
                    if not alive(n):
                        return
                    if real(n):
                        v.wait_ge(x_in[b], 16 * i + 16)
                        for k in range(2):
                            d = v.bn_stats(stat[:, k, :], x[:, b, k, :])
                    if real(n - LAG):
                        v.wait_ge(summed, n - LAG + 1)
                        for k in range(2):
                            d = v.bn_stats(stat[:, 2 + k, :], z[:, b, k, :])
                    d.then_inc(vec, 1)
                    count = VEC * n + 1
                    need_apart(v, vec, count + 1)
                    for k in range(4):
                        d = v.bn_aggr(mom[:, k, :], stat[:, k, :])
                    d.then_inc(vec, 1)
                    v.wait_ge(vec, count + 2)
                    v.tensor_scalar(var[:], mom[:, :, 1], EPS, None, ALU.add).then_inc(vec, 1)
                    v.wait_ge(vec, count + 3)
                    need(v, normed, min(n - 1, STEPS) if isinstance(n, int) else n - 1)
                    need(v, final, n - 1 - LAG)
                    reciprocal_sqrt(v, var[:], rstd[:, b], bits[:], half[:], vec, count + 3)
                    v.scalar_tensor_tensor(out=shift[:, b], in0=mom[:, :, 0], scalar=-1.0, in1=rstd[:, b],
                                           op0=ALU.mult, op1=ALU.mult).then_inc(vec, 1)

                node_steps(v, emit)

            @block.scalar
            def _(act):
                def emit(n, b, i):
                    if not alive(n):
                        return
                    act.wait_ge(vec, VEC * (n + 1) + 1)
                    if real(n):
                        need(act, gained, n)
                        for k in range(2):
                            d = act.activation(yn[:, k, :], x[:, b, k, :], ACT.Identity, bias=shift[:, b, k:k + 1],
                                               scale=rstd[:, b, k:k + 1])
                        d.then_inc(normed, 1)
                    if real(n - LAG):
                        need(act, stored[b], 16 * (i - 1))
                        for k in range(2):
                            d = act.activation(out[:, b, k, :], z[:, b, k, :], ACT.Identity, bias=shift[:, b, 2 + k:3 + k],
                                               scale=rstd[:, b, 2 + k:3 + k])
                        d.then_inc(final, 1)
                        act.wait_ge(final, n - LAG + 1)
                        if isinstance(n, int) and n - LAG == STEPS - 1:
                            act.dma_start(g.out[N - left:N, :], out[0:left, b, 0, :]).then_inc(stored[b], 16)
                        else:
                            act.dma_start(two_windows(g.out, n - LAG), out[:, b]).then_inc(stored[b], 16)

                node_steps(act, emit)
                act.wait_ge(stored[0], 16 * ((STEPS + 1) // 2))
                act.wait_ge(stored[1], 16 * (STEPS // 2))

            @block.gpsimd
            def _(pool):
                pool.wait_ge(w_in, 32)

                def emit(n, b, i):
                    if real(n):
                        pool.wait_ge(x1_in[b], 16 * i + 16)
                        need(pool, summed, n)
                        nc.gpsimd.tensor_tensor(x1b[:], x1[:, b], both(rows[:, 1]), ALU.add).then_inc(shifted, 1)
                        pool.wait_ge(normed, n + 1)
                        nc.gpsimd.tensor_tensor(yg[:], yn[:], both(rows[:, 0]), ALU.mult).then_inc(gained, 1)
                        pool.wait_ge(shifted, n + 1)
                        pool.wait_ge(gained, n + 1)
                        need(pool, final, n - 1)
                        nc.gpsimd.tensor_tensor(z[:, b], yg[:], x1b[:], ALU.add).then_inc(summed, 1)

                node_steps(pool, emit)

        end_phase(nc, sems)


INPUTS = ["x", "src", "dst", "edge_type_3", "node_type_4", "L0_gnn_W", "L1_gnn_W_Q", "L1_gnn_W_K", "L1_gnn_W_V",
          "L1_gnn_W_E", "L1_gnn_mu", "L1_gnn_Wo", "L1_gnn_bo", "L1_gnn_ln1_g", "L1_gnn_ln1_b", "L1_gnn_ln2_g",
          "L1_gnn_ln2_b", "L1_gnn_w1", "L1_gnn_b1", "L1_gnn_w2", "L1_gnn_b2", "L1_gnn_out_g", "L1_gnn_out_b"]


def gnn_kernel(nc, ins, out):
    g = Shared()
    (g.x, g.src, g.dst, g.edge_type, g.node_type, g.gcn_w, g.w_q, g.w_k, g.w_v, g.w_e, g.mu, g.wo, g.bo, g.ln1_g,
     g.ln1_b, g.ln2_g, g.ln2_b, g.w1, g.b1, g.w2, g.b2, g.out_g, g.out_b) = ins
    g.out = out

    def dram(name, shape, dt=F32):
        return nc.dram_tensor(name, shape, dt, kind="Internal").ap()

    g.x_d = dram("x_state", (NPAD, D))
    g.x1_d = dram("x_first", (NPAD, D))
    g.xs_d = dram("x_scaled", (NPAD, D))
    g.tab_d = dram("kv_table", (EDGE_TYPES, NPAD, ROW))
    g.idx_d = dram("row_indices", (2, BLOCKS, P, TILES), I32)
    g.place_d = dram("places", (BLOCKS, P, TILES))
    g.rec_d = dram("block_records", (BLOCKS, P, REC))
    with ExitStack() as ctx:
        def sb(name, shape, dt=F32):
            return ctx.enter_context(nc.sbuf_tensor(name, shape, dt))

        g.ps = ctx.enter_context(nc.psum_tensor("ps", [P, 8, 512], F32))
        g.ident = sb("ident", [P, P])
        g.minus_ident = sb("minus_ident", [P, P])
        g.iota = sb("iota", [P, P])
        g.ones = sb("ones", [P, P])
        g.zeros = sb("zeros", [P, D])
        g.pair_iota = sb("pair_iota", [P, 4])
        g.same_head = sb("same_head", [P, P])
        g.tile_hot = sb("tile_hot", [P, TILES])
        g.type_hot = sb("type_hot", [P, WINDOWS, NODE_TYPES])
        g.dis = sb("dis", [P, WINDOWS])
        g.keep = sb("keep", [P, PAIRS])
        g.shifts = [0, LAG_COPY, LAG_ADD]
        g.window_rows = sb("window_rows", [P, 3, 480], I32)
        g.sums = sb("sums", [P, (WINDOWS + 1) * UROW])
        g.landed = [ctx.enter_context(nc.semaphore(f"landed{k}")) for k in range(RING)]
        constants(nc, g)
        with nc.sbuf_tensor("before", [P, BLOCKS], F32) as g.before, \
                nc.sbuf_tensor("minus_place", [P, 2 * PAIRS], F32) as g.minus_place, \
                nc.sbuf_tensor("key", [P, 2 * PAIRS], F32) as g.key:
            with nc.sbuf_tensor("idx", [P, 2, BLOCKS, TILES], I32) as g.idx:
                index_pairs(nc, g)
            gcn_edges(nc, g)
        gcn_nodes(nc, g)
        with nc.Fori(0, LAYERS) as layer:
            project(nc, g, layer)
            with ExitStack() as weights:
                nw = NodeWeights(nc, weights)
                attention_edges(nc, g, layer, nw)
                attention_nodes(nc, g, layer, nw)
        last_norms(nc, g)


def kernel(**inputs):
    import numpy as _np
    import concourse.bacc as _bacc
    from concourse import mybir as _mybir
    from concourse.bass_utils import run_bass_kernel_spmd as _run

    nc = _bacc.Bacc("TRN2", target_bir_lowering=False, num_devices=1)
    arrays, args = {}, []
    for name in INPUTS:
        a = _np.ascontiguousarray(inputs[name])
        arrays[f"in_{name}"] = a
        args.append(nc.dram_tensor(f"in_{name}", a.shape, _mybir.dt.from_np(a.dtype), kind="ExternalInput").ap())
    out = nc.dram_tensor("out_0", (N, D), _mybir.dt.float32, kind="ExternalOutput").ap()
    gnn_kernel(nc, args, out)
    r = _run(nc, [arrays], core_ids=[0])
    return r.results[0]["out_0"]
```
